# Optimizing a Trainium2 kernel written in Bass

```python
import numpy as np
import jax
import jax.numpy as jnp

def _softmax(x, axis=-1):
    return jax.nn.softmax(x, axis=axis)

def _gelu(x):
    return jax.nn.gelu(x, approximate=True)

def _silu(x):
    return jax.nn.silu(x)

def _sigmoid(x):
    return jax.nn.sigmoid(x)

def _layernorm(x, axis=-1, eps=1e-05):
    m = jnp.mean(x, axis=axis, keepdims=True)
    v = jnp.var(x, axis=axis, keepdims=True)
    return (x - m) / jnp.sqrt(v + eps)

def _scatter_add(tgt, idx, src, axis=0):
    return tgt.at[idx].add(src)

def _segment_sum(src, seg, n):
    return jax.ops.segment_sum(src, seg, n)
kernel_name = 'mk_lm_tower_d1_tok_ids512_r4_678132'

def setup_inputs(seed: int=0):
    np.random.seed(seed)
    _w = jnp.asarray

    def _rec_inputs():
        import jax
        import jax.numpy as jnp
        _rk = jax.random.key(seed)
        x = jax.random.randint(jax.random.fold_in(_rk, 1), (16, 256), 0, 50257, jnp.int32)
        return x
    x = _rec_inputs()

    def _L0_tok_setup():
        import jax, jax.numpy as jnp
        import numpy as np
        VOCAB = 50257
        FEAT = 128
        EPS = 1e-12
        key = jax.random.key(seed)
        k1, k2, k3 = jax.random.split(key, 3)
        token_ids = jax.random.randint(k1, (32, 1024), 0, VOCAB)
        W = jax.random.normal(k2, (FEAT, VOCAB), dtype=jnp.float32) * 0.02
        b = jax.random.normal(k3, (FEAT,), dtype=jnp.float32) * 0.02
        return {'token_ids': token_ids, 'W': W, 'b': b}
    _L0_tok_all = _L0_tok_setup()
    _L0_tok_in = {k: v for k, v in _L0_tok_all.items() if k in ('W', 'b')}
    del _L0_tok_all

    def _L0_attn_setup():
        import jax, jax.numpy as jnp
        import numpy as np
        H, KVH, HD, DN, DR = (8, 2, 64, 32, 32)
        EPS = 1e-06
        ROPE_BASE = 500000.0

        def _rms(x, w):
            return w * (x * jax.lax.rsqrt(jnp.mean(x * x, axis=-1, keepdims=True) + EPS))

        def _rope_tables(T):
            inv_freq = 1.0 / ROPE_BASE ** (np.arange(0, DR, 2, dtype=np.float32) / DR)
            freqs = np.outer(np.arange(T, dtype=np.float32), inv_freq)
            emb = np.concatenate([freqs, freqs], axis=-1)
            return (jnp.asarray(np.cos(emb)), jnp.asarray(np.sin(emb)))

        def _apply_rope(x, cos, sin):
            x1, x2 = jnp.split(x, 2, axis=-1)
            rot = jnp.concatenate([-x2, x1], axis=-1)
            return x * cos[None, None] + rot * sin[None, None]
        key = jax.random.key(seed)
        ks = jax.random.split(key, 10)
        std = 0.02
        mup = (256.0 / 512.0) ** 0.5
        return {'x': jax.random.normal(ks[0], (4, 512, 128), jnp.float32), 'W_DQ': jax.random.normal(ks[1], (128, 64), jnp.float32) * std, 'W_UQ': jax.random.normal(ks[2], (64, H * DN), jnp.float32) * std, 'W_QR': jax.random.normal(ks[3], (64, H * DR), jnp.float32) * std, 'W_DKV': jax.random.normal(ks[4], (128, 128), jnp.float32) * std, 'W_UK': jax.random.normal(ks[5], (128, KVH * DN), jnp.float32) * std, 'W_UV': jax.random.normal(ks[6], (128, KVH * HD), jnp.float32) * std, 'W_KR': jax.random.normal(ks[7], (128, KVH * DR), jnp.float32) * std, 'W_VR': jax.random.normal(ks[8], (128, H * HD), jnp.float32) * std * mup, 'W_O': jax.random.normal(ks[9], (H * HD, 128), jnp.float32) * std * mup, 'q_ln_w': jnp.ones((64,), jnp.float32), 'kv_ln_w': jnp.ones((128,), jnp.float32), 'q_head_norm_w': jnp.ones((HD,), jnp.float32), 'k_head_norm_w': jnp.ones((HD,), jnp.float32)}
    _L0_attn_all = _L0_attn_setup()
    _L0_attn_in = {k: v for k, v in _L0_attn_all.items() if k in ('W_DQ', 'W_UQ', 'W_QR', 'W_DKV', 'W_UK', 'W_UV', 'W_KR', 'W_VR', 'W_O', 'q_ln_w', 'kv_ln_w', 'q_head_norm_w', 'k_head_norm_w')}
    del _L0_attn_all

    def _L0_ffn_setup():
        import jax, jax.numpy as jnp
        import numpy as np
        D = 128
        E = 8
        K = 2
        EXP = 4
        LN_EPS = 1e-05
        key = jax.random.key(seed)
        ks = jax.random.split(key, 8)
        B, T = (8, 512)
        Dh = D * EXP
        x = jax.random.normal(ks[0], (B, T, D), dtype=jnp.float32)
        ln_g = jnp.ones((D,), dtype=jnp.float32)
        ln_b = jnp.zeros((D,), dtype=jnp.float32)
        lim_r = np.sqrt(6.0 / (D + E)).astype(np.float32)
        w_r = jax.random.uniform(ks[1], (E, D), dtype=jnp.float32, minval=-lim_r, maxval=lim_r)
        b_r = jnp.zeros((E,), dtype=jnp.float32)
        lim1 = np.sqrt(6.0 / (D + Dh)).astype(np.float32)
        W1 = jax.random.uniform(ks[2], (E, D, Dh), dtype=jnp.float32, minval=-lim1, maxval=lim1)
        b1 = jnp.zeros((E, Dh), dtype=jnp.float32)
        W2 = jax.random.uniform(ks[3], (E, Dh, D), dtype=jnp.float32, minval=-lim1, maxval=lim1)
        b2 = jnp.zeros((E, D), dtype=jnp.float32)
        return {'x': x, 'ln_g': ln_g, 'ln_b': ln_b, 'w_r': w_r, 'b_r': b_r, 'W1': W1, 'b1': b1, 'W2': W2, 'b2': b2}
    _L0_ffn_all = _L0_ffn_setup()
    _L0_ffn_in = {k: v for k, v in _L0_ffn_all.items() if k in ('ln_g', 'ln_b', 'w_r', 'b_r', 'W1', 'b1', 'W2', 'b2')}
    del _L0_ffn_all
    return {'x': x, 'L0_tok_W': _L0_tok_in['W'], 'L0_tok_b': _L0_tok_in['b'], 'L0_attn_W_DQ': _L0_attn_in['W_DQ'], 'L0_attn_W_UQ': _L0_attn_in['W_UQ'], 'L0_attn_W_QR': _L0_attn_in['W_QR'], 'L0_attn_W_DKV': _L0_attn_in['W_DKV'], 'L0_attn_W_UK': _L0_attn_in['W_UK'], 'L0_attn_W_UV': _L0_attn_in['W_UV'], 'L0_attn_W_KR': _L0_attn_in['W_KR'], 'L0_attn_W_VR': _L0_attn_in['W_VR'], 'L0_attn_W_O': _L0_attn_in['W_O'], 'L0_attn_q_ln_w': _L0_attn_in['q_ln_w'], 'L0_attn_kv_ln_w': _L0_attn_in['kv_ln_w'], 'L0_attn_q_head_norm_w': _L0_attn_in['q_head_norm_w'], 'L0_attn_k_head_norm_w': _L0_attn_in['k_head_norm_w'], 'L0_ffn_ln_g': _L0_ffn_in['ln_g'], 'L0_ffn_ln_b': _L0_ffn_in['ln_b'], 'L0_ffn_w_r': _L0_ffn_in['w_r'], 'L0_ffn_b_r': _L0_ffn_in['b_r'], 'L0_ffn_W1': _L0_ffn_in['W1'], 'L0_ffn_b1': _L0_ffn_in['b1'], 'L0_ffn_W2': _L0_ffn_in['W2'], 'L0_ffn_b2': _L0_ffn_in['b2']}

def reference(x, L0_tok_W, L0_tok_b, L0_attn_W_DQ, L0_attn_W_UQ, L0_attn_W_QR, L0_attn_W_DKV, L0_attn_W_UK, L0_attn_W_UV, L0_attn_W_KR, L0_attn_W_VR, L0_attn_W_O, L0_attn_q_ln_w, L0_attn_kv_ln_w, L0_attn_q_head_norm_w, L0_attn_k_head_norm_w, L0_ffn_ln_g, L0_ffn_ln_b, L0_ffn_w_r, L0_ffn_b_r, L0_ffn_W1, L0_ffn_b1, L0_ffn_W2, L0_ffn_b2):
    import jax
    import jax.numpy as jnp

    def _L0_tok_ref(token_ids, W, b):
        import jax, jax.numpy as jnp
        import numpy as np
        VOCAB = 50257
        FEAT = 128
        EPS = 1e-12
        feats = W.T[token_ids] + b
        norm = jnp.sqrt(jnp.sum(feats * feats, axis=-1, keepdims=True))
        return feats / jnp.maximum(norm, EPS)

    def _L0_attn_ref(x, W_DQ, W_UQ, W_QR, W_DKV, W_UK, W_UV, W_KR, W_VR, W_O, q_ln_w, kv_ln_w, q_head_norm_w, k_head_norm_w):
        import jax, jax.numpy as jnp
        import numpy as np
        H, KVH, HD, DN, DR = (8, 2, 64, 32, 32)
        EPS = 1e-06
        ROPE_BASE = 500000.0

        def _rms(x, w):
            return w * (x * jax.lax.rsqrt(jnp.mean(x * x, axis=-1, keepdims=True) + EPS))

        def _rope_tables(T):
            inv_freq = 1.0 / ROPE_BASE ** (np.arange(0, DR, 2, dtype=np.float32) / DR)
            freqs = np.outer(np.arange(T, dtype=np.float32), inv_freq)
            emb = np.concatenate([freqs, freqs], axis=-1)
            return (jnp.asarray(np.cos(emb)), jnp.asarray(np.sin(emb)))

        def _apply_rope(x, cos, sin):
            x1, x2 = jnp.split(x, 2, axis=-1)
            rot = jnp.concatenate([-x2, x1], axis=-1)
            return x * cos[None, None] + rot * sin[None, None]
        B, T, D = x.shape
        cos, sin = _rope_tables(T)
        c_q = _rms(x @ W_DQ, q_ln_w)
        q_nope = (c_q @ W_UQ).reshape(B, T, H, DN).transpose(0, 2, 1, 3)
        q_rope = (c_q @ W_QR).reshape(B, T, H, DR).transpose(0, 2, 1, 3)
        c_kv = _rms(x @ W_DKV, kv_ln_w)
        k_nope = (c_kv @ W_UK).reshape(B, T, KVH, DN).transpose(0, 2, 1, 3)
        v = (c_kv @ W_UV).reshape(B, T, KVH, HD).transpose(0, 2, 1, 3)
        k_rope = (x @ W_KR).reshape(B, T, KVH, DR).transpose(0, 2, 1, 3)
        q_rope = _apply_rope(q_rope, cos, sin)
        k_rope = _apply_rope(k_rope, cos, sin)
        q = jnp.concatenate([q_nope, q_rope], axis=-1)
        k = jnp.concatenate([k_nope, k_rope], axis=-1)
        q = _rms(q, q_head_norm_w)
        k = _rms(k, k_head_norm_w)
        g = H // KVH
        k = jnp.repeat(k, g, axis=1)
        v = jnp.repeat(v, g, axis=1)
        scores = jnp.einsum('bhqd,bhkd->bhqk', q, k) * HD ** (-0.5)
        mask = jnp.tril(jnp.ones((T, T), dtype=bool))
        scores = jnp.where(mask, scores, -jnp.inf)
        attn_w = jax.nn.softmax(scores.astype(jnp.float32), axis=-1).astype(q.dtype)
        attn_out = jnp.einsum('bhqk,bhkd->bhqd', attn_w, v)
        v_res = (x @ W_VR).reshape(B, T, H, HD).transpose(0, 2, 1, 3)
        attn_out = attn_out + v_res
        out = attn_out.transpose(0, 2, 1, 3).reshape(B, T, H * HD)
        return out @ W_O

    def _L0_ffn_ref(x, ln_g, ln_b, w_r, b_r, W1, b1, W2, b2):
        import jax, jax.numpy as jnp
        import numpy as np
        D = 128
        E = 8
        K = 2
        EXP = 4
        LN_EPS = 1e-05
        B, T, d = x.shape
        mu = jnp.mean(x, axis=-1, keepdims=True)
        var = jnp.mean(jnp.square(x - mu), axis=-1, keepdims=True)
        h = (x - mu) * jax.lax.rsqrt(var + LN_EPS) * ln_g + ln_b
        logits = jnp.einsum('btd,ed->bte', h, w_r) + b_r
        topk_vals, topk_idx = jax.lax.top_k(logits, K)
        gates = jax.nn.softmax(topk_vals, axis=-1)
        hf = h.reshape(B * T, d)
        hid = jax.nn.gelu(jnp.einsum('nd,edf->nef', hf, W1) + b1, approximate=False)
        expert_stack = jnp.einsum('nef,efd->ned', hid, W2) + b2
        idx_flat = topk_idx.reshape(B * T, K)
        gates_flat = gates.reshape(B * T, K)
        gathered = jnp.take_along_axis(expert_stack, idx_flat[:, :, None], axis=1)
        mixed = jnp.sum(gathered * gates_flat[:, :, None], axis=1).reshape(B, T, d)
        return x + mixed
    h = _L0_tok_ref(x, L0_tok_W, L0_tok_b)
    h = h + _L0_attn_ref(_layernorm(h, axis=-1), L0_attn_W_DQ, L0_attn_W_UQ, L0_attn_W_QR, L0_attn_W_DKV, L0_attn_W_UK, L0_attn_W_UV, L0_attn_W_KR, L0_attn_W_VR, L0_attn_W_O, L0_attn_q_ln_w, L0_attn_kv_ln_w, L0_attn_q_head_norm_w, L0_attn_k_head_norm_w)
    h = h + _L0_ffn_ref(_layernorm(h, axis=-1), L0_ffn_ln_g, L0_ffn_ln_b, L0_ffn_w_r, L0_ffn_b_r, L0_ffn_W1, L0_ffn_b1, L0_ffn_W2, L0_ffn_b2)
    return h

_drawn_inputs = setup_inputs


def setup_inputs(seed=0):
    import zlib

    import numpy as np

    out = dict(_drawn_inputs(seed))
    spreads = {'L0_attn_q_ln_w': (1.0, 0.6),
     'L0_attn_kv_ln_w': (1.0, 0.2),
     'L0_attn_q_head_norm_w': (1.0, 0.6),
     'L0_attn_k_head_norm_w': (1.0, 0.6),
     'L0_ffn_ln_g': (1.0, 0.2),
     'L0_ffn_ln_b': (0.0, 0.1),
     'L0_ffn_b_r': (0.0, 0.1),
     'L0_ffn_b1': (0.0, 0.1),
     'L0_ffn_b2': (0.0, 0.1)}
    factors = {}
    for name, (base, spread) in spreads.items():
        noise = np.random.default_rng([zlib.crc32(name.encode()), seed]).standard_normal(out[name].shape)
        drawn = base * np.exp(spread * noise) if base else spread * noise
        out[name] = jnp.asarray(drawn.astype(out[name].dtype))
    for name, factor in factors.items():
        out[name] = (out[name] * factor).astype(out[name].dtype)
    return out
```

```python
import concourse.bass as bass
from concourse import mybir
from contextlib import ExitStack

F32 = mybir.dt.float32
BF16 = mybir.dt.bfloat16
I32 = mybir.dt.int32
U32 = mybir.dt.uint32
ALU = mybir.AluOpType
ACT = mybir.ActivationFunctionType
AX = mybir.AxisListType

P = 128
D = 128
B, T = 16, 256
NT = T // P
TILES = B * NT
VOCAB = 50257
H, KVH, HD, DN, DR = 8, 2, 64, 32, 32
G = H // KVH
RQ, RKV = 64, 128

CW = 1024
CJ = CW // P
CHUNKS = VOCAB // CW
TAIL = VOCAB - CHUNKS * CW
RING = 8
ROUNDS = CHUNKS // RING
assert CHUNKS == ROUNDS * RING + 1 and TAIL <= P

E, K, FF = 8, 2, 512
FC = FF // P
N = B * T
GT = 2
GR = GT * P
REGION = N + GR
NJ = N * K // GR + E
XR = 4
ROW = D + 4
GATE, DEST = D, D + 1
assert NJ % XR == 0 and GR & (GR - 1) == 0

UNITS = [(0, 0, 0, 4), (0, 1, 0, 4), (1, 0, 0, 2), (1, 0, 2, 2), (1, 1, 0, 2), (1, 1, 2, 2)]
NU = len(UNITS)


def wait(eng, sem, value):
    if isinstance(value, int) and value <= 0:
        return
    eng.wait_ge(sem, value)


def stand_alone(eng, sem):
    eng.sem_inc(sem, 1)


def tower_kernel(nc, x, tok_W, tok_b, W_DQ, W_UQ, W_QR, W_DKV, W_UK, W_UV, W_KR, W_VR, W_O, q_ln_w,
                 kv_ln_w, qh_w, kh_w, ln_g, ln_b, w_r, b_r, W1, b1, W2, b2, rope, table,
                 xs, ys, out):
    with ExitStack() as ctx:
        def sb(name, shape, dt=F32):
            return ctx.enter_context(nc.sbuf_tensor(name, shape, dt))

        def sem(name):
            return ctx.enter_context(nc.semaphore(name))

        w_in = sb("w_in", [P, RING, CW])
        w_out = sb("w_out", [P, RING, CJ, D])
        ident = sb("ident", [P, P])
        identb = sb("identb", [P, P], BF16)
        masks = sb("masks", [P, 2, 512], BF16)
        maskf = sb("maskf", [P, P])
        ids = sb("ids", [P, TILES], I32)
        ids_now = sb("ids_now", [P, 2, NT], I32)
        tokb = sb("tokb", [P, D])
        cossin = sb("cossin", [P, 2, NT, DR])
        wdq = sb("wdq", [P, RQ])
        wdkv = sb("wdkv", [P, RKV])
        wkr = sb("wkr", [P, KVH * DR])
        wq_raw = sb("wq_raw", [RQ, G, KVH, HD])
        wq = sb("wq", [RQ, G * KVH * HD])
        wkv_raw = sb("wkv_raw", [P, KVH * DN + KVH * HD])
        wkv = sb("wkv", [P, KVH * DN + KVH * HD])
        wvr = sb("wvr", [P, G, KVH, HD])
        wvrT = sb("wvrT", [P, G, D])
        wo = sb("wo", [P, G, D])
        wvo = sb("wvo", [P, D])
        qln = sb("qln", [RQ, 1])
        kvln = sb("kvln", [P, 1])
        hw2 = sb("hw2", [P, 2, HD])
        khw = sb("khw", [P, HD])
        mean_w = sb("mean_w", [P, 2])
        neg_half = sb("neg_half", [P, 16])
        gat = sb("gat", [P, 2, NT, D])
        f = sb("f", [P, NT, D])
        bst = sb("bst", [P, NT, 6])
        mv = sb("mv", [P, NT, 2])
        est = sb("est", [P, 10, NT])
        hall = sb("hall", [P, TILES, D])
        xn = sb("xn", [P, 2, NT, D])
        xT = sb("xT", [P, 2, T])
        sqc = sb("sqc", [P, 2, T])
        cqT = sb("cqT", [RQ, T])
        ckvT = sb("ckvT", [P, T])
        em = sb("em", [P, NT, 2])
        skv = sb("skv", [P, NT])
        epsq = sb("epsq", [P, NT])
        qt = sb("qt", [P, NT, G, KVH, HD])
        kt = sb("kt", [P, NT, KVH, HD])
        v = sb("v", [P, 2, NT, KVH * HD])
        rope_a = sb("rope_a", [P, NT, H, DR])
        rope_b = sb("rope_b", [P, NT, H, DR])
        krope_a = sb("krope_a", [P, NT, KVH, DR])
        krope_b = sb("krope_b", [P, NT, KVH, DR])
        qsq = sb("qsq", [P, NT, H, HD])
        qss = sb("qss", [P, NT, H])
        rqv = sb("rqv", [P, NT, H])
        rq = sb("rq", [P, 2, NT, G, KVH])
        ksq = sb("ksq", [P, NT, KVH, HD])
        kss = sb("kss", [P, NT * KVH])
        rkv = sb("rkv", [P, NT * KVH])
        rk = sb("rk", [P, NT * KVH])
        qT = sb("qT", [P, 2, NT, G, P])
        kT = sb("kT", [P, 2, T])
        negmax = sb("negmax", [P, NU, G])
        nbias = sb("nbias", [P, NU, G])
        pm = sb("pm", [P, 2, 512])
        rsum = sb("rsum", [P, NT, G, KVH])
        rinv = sb("rinv", [P, NT, G, KVH])
        rwide = sb("rwide", [P, NT, G, KVH * HD])
        rb = sb("rb", [P, NT, 512])
        pt0 = sb("pt0", [P, KVH, G, P])
        pt1 = sb("pt1", [P, KVH, G, NT, P])
        on = sb("on", [P, NT, G, P])

        iota8 = sb("iota8", [P, E])
        region8 = sb("region8", [P, E])
        before = sb("before", [P, P])
        beforeb = sb("beforeb", [P, P], BF16)
        onesb = sb("onesb", [P, P], BF16)
        lng = sb("lng", [P, 1])
        lnb = sb("lnb", [P, 1])
        wrT = sb("wrT", [P, E])
        br = sb("br", [P, E])
        bst2 = sb("bst2", [P, NT, 6])
        mv2 = sb("mv2", [P, NT, 2])
        rst = sb("rst", [P, 10, NT])
        row = sb("row", [P, 2, NT, K, ROW])
        dest = sb("dest", [P, NT, K])
        hfT = sb("hfT", [P, T])
        lg = sb("lg", [P, NT, E])
        mx8 = sb("mx8", [P, NT, 8])
        ix8 = sb("ix8", [P, NT, 8], U32)
        ixf = sb("ixf", [P, NT, K])
        chosen = sb("chosen", [P, NT, K, E])
        both = sb("both", [P, NT, E], BF16)
        seen = sb("seen", [P, E], BF16)
        dlog = sb("dlog", [P, NT])
        eg = sb("eg", [P, NT])
        eg1 = sb("eg1", [P, NT])
        pos = sb("pos", [P, NT, E])
        posk = sb("posk", [P, NT, K, E])
        slotf = sb("slotf", [P, NT * K])
        slot = sb("slot", [P, 2, NT * K], I32)
        cnt = sb("cnt", [1, E])
        cnti = sb("cnti", [1, E], I32)
        cntt = sb("cntt", [1, E], I32)
        ntile = sb("ntile", [1, E])
        tend = sb("tend", [1, E])
        tbase = sb("tbase", [1, E])
        zero8 = sb("zero8", [1, E])
        iotaj = sb("iotaj", [1, NJ])
        je = sb("je", [1, NJ, E])
        jexp = sb("jexp", [1, NJ])
        jvalid = sb("jvalid", [1, NJ])
        jstart = sb("jstart", [1, NJ])
        start_i = sb("start_i", [1, NJ], I32)
        expert_i = sb("expert_i", [1, NJ], I32)
        padrow = sb("padrow", [1, E])
        pad_i = sb("pad_i", [1, E], I32)
        padding = sb("padding", [P, GT, ROW])
        w_flat = w_out[:, :, :, :].rearrange("p u j d -> p (u j d)")
        w2s = w_flat[:, 0:E * FC * D].rearrange("p (e c d) -> p e c d", e=E, c=FC)
        w1c = w_flat[:, E * FC * D:E * FC * D + XR * FF].rearrange("p (r f) -> p r f", r=XR)
        x_flat = w_in[:, :, :].rearrange("p u c -> p (u c)")
        at = [0]

        def carve(n):
            at[0] += n
            return x_flat[:, at[0] - n:at[0]]

        rows = carve(XR * GT * ROW).rearrange("p (r t c) -> p r t c", r=XR, t=GT)
        hT = carve(2 * GR).rearrange("p (r n) -> p r n", r=2)
        hid = carve(2 * FC * GR).rearrange("p (r c n) -> p r c n", r=2, c=FC)
        yt = carve(2 * GT * D).rearrange("p (r t d) -> p r t d", r=2, t=GT)
        yb = carve(XR * GT * D).rearrange("p (r t d) -> p r t d", r=XR, t=GT)
        b2c = carve(XR * D).rearrange("p (r d) -> p r d", r=XR)
        b1s = sb("b1s", [P, E, FC])
        b2s = sb("b2s", [P, E, D])
        b1c = sb("b1c", [P, XR, FC])
        where = sb("where", [P, XR, GT], I32)

        banks = [ctx.enter_context(nc.psum_tensor(f"bank{i}", [P, 512], F32)) for i in range(8)]
        S = banks[0:3]
        TB = banks[3:5]
        O, M0, M1 = banks[5:8]
        HID, XT, Y = (banks[0:2], banks[2:4]), banks[4:6], banks[6:8]

        QT = TILES // 4
        y_parts = w_in[:, :, :].rearrange("p u c -> p (u c)").rearrange("p (k c t d) -> p k c t d", k=K, c=4, t=QT)

        chunk_in = [sem(f"chunk_in{u}") for u in range(RING)]
        chunk_out = [sem(f"chunk_out{u}") for u in range(RING)]
        turned = sem("turned")
        even_copied = sem("even_copied")
        odd_copied = sem("odd_copied")
        consts_in = sem("consts_in")
        ids_in = sem("ids_in")
        pool_init = sem("pool_init")
        dve_init = sem("dve_init")
        setup_pe = sem("setup_pe")
        setup_act = sem("setup_act")
        rows_in = [sem("rows_in0"), sem("rows_in1")]
        ids_copied = sem("ids_copied")
        e_pool = sem("e_pool")
        e_dve = sem("e_dve")
        x_ready = sem("x_ready")
        f_ready = sem("f_ready")
        mv_ready = sem("mv_ready")
        pe_xT = sem("pe_xT")
        act_xT = sem("act_xT")
        pe_c = sem("pe_c")
        act_sq = sem("act_sq")
        dve_c = sem("dve_c")
        pe_stat = sem("pe_stat")
        pe_kv = sem("pe_kv")
        dve_stat = sem("dve_stat")
        skv_ready = sem("skv_ready")
        dve_kv = sem("dve_kv")
        p_pool = sem("p_pool")
        pe_q = sem("pe_q")
        act_q = sem("act_q")
        dve_rope = sem("dve_rope")
        q_ready = sem("q_ready")
        ksq_ready = sem("ksq_ready")
        kss_ready = sem("kss_ready")
        qss_ready = sem("qss_ready")
        rq_ready = sem("rq_ready")
        k_ready = sem("k_ready")
        pe_qT = sem("pe_qT")
        act_qT = sem("act_qT")
        pe_kT = sem("pe_kT")
        act_kT = sem("act_kT")
        scored = sem("scored")
        max_done = sem("max_done")
        bias_ready = sem("bias_ready")
        exped = sem("exped")
        t_full = [sem("t_full0"), sem("t_full1")]
        t_free = [sem("t_free0"), sem("t_free1")]
        rinv_done = sem("rinv_done")
        rinv_ready = sem("rinv_ready")
        pv_done = [sem("pv_done0"), sem("pv_done1")]
        on_ready = [sem("on_ready0"), sem("on_ready1")]
        pe_wo = sem("pe_wo")
        h_added = sem("h_added")
        stored = sem("stored")
        weights_in = sem("weights_in")
        r_stats = sem("r_stats")
        mv2_ready = sem("mv2_ready")
        r_pool = sem("r_pool")
        coef_ready = sem("coef_ready")
        hh_ready = sem("hh_ready")
        base_ready = sem("base_ready")
        pe_h = sem("pe_h")
        act_h = sem("act_h")
        pe_logits = sem("pe_logits")
        logits_copied = sem("logits_copied")
        r_dve = sem("r_dve")
        g_dve = sem("g_dve")
        dlog_ready = sem("dlog_ready")
        eg_ready = sem("eg_ready")
        both_ready = sem("both_ready")
        pe_rank = sem("pe_rank")
        rank_copied = sem("rank_copied")
        slot_ready = sem("slot_ready")
        scattered = [sem("scattered0"), sem("scattered1")]
        row_full = sem("row_full")
        pe_count = sem("pe_count")
        c_dve = sem("c_dve")
        t_dve = sem("t_dve")
        tables_ready = sem("tables_ready")
        padded = sem("padded")
        group_in = [sem(f"group_in{b}") for b in range(XR)]
        w1_in = [sem(f"w1_in{b}") for b in range(XR)]
        biases_ready = sem("biases_ready")
        x_turned = sem("x_turned")
        hT_ready = sem("hT_ready")
        hidden_done = sem("hidden_done")
        hid_ready = sem("hid_ready")
        y_done = sem("y_done")
        y_biased = sem("y_biased")
        y_ready = sem("y_ready")
        y_out = [sem(f"y_out{b}") for b in range(XR)]
        y_in = [sem(f"y_in{c}") for c in range(4)]
        y_add = sem("y_add")
        y_sum = sem("y_sum")
        passed = sem("passed")

        block = ctx.enter_context(nc.Block())

        SMALL = 24

        def chunk_rows(n):
            return table[bass.ds(n * CW, CW), :].rearrange("(p j) d -> p (j d)", j=CJ)

        T_USES = [("p", 0), ("p", 1), ("r", 0), ("p", 2), ("p", 3), ("p", 4), ("p", 5), ("r", 1)]

        def t_use(kind, n):
            k = T_USES.index((kind, n))
            return k % 2, k // 2

        def pt_evacuate(eng, copy, s, u):
            t, kv, j0, n = UNITS[u]
            bank, use = t_use("p", u)
            eng.wait_ge(t_full[bank], 4 * s + use + 1)
            wait(eng, pv_done[t], s)
            if t == 0:
                dst = pt0[:, kv].rearrange("p j q -> p (j q)")
            else:
                dst = pt1[:, kv, j0:j0 + n].rearrange("p j k q -> p (j k q)")
            copy(dst, TB[bank][:, :]).then_inc(t_free[bank], 1)

        @block.sync
        def _(sp):
            def load(n, u):
                sp.dma_start(w_in[:, u, :], tok_W[:, bass.ds(n * CW, CW)]).then_inc(chunk_in[u], 16)

            def store(n, u):
                sp.wait_ge(even_copied, n + 1)
                sp.wait_ge(odd_copied, n + 1)
                sp.dma_start(chunk_rows(n), w_out[:, u].rearrange("p j d -> p (j d)")).then_inc(chunk_out[u], 16)

            for u in range(RING):
                load(u, u)
            with sp.Fori(0, ROUNDS - 1) as i:
                for u in range(RING):
                    store(i * RING + u, u)
                    load(i * RING + u + RING, u)
            for u in range(RING):
                n = (ROUNDS - 1) * RING + u
                store(n, u)
                if u == 0:
                    load(n + RING, u)
                if u == 1:
                    sp.dma_start(w_in[:, u, 0:TAIL], tok_W[:, CHUNKS * CW:VOCAB]).then_inc(chunk_in[u], 16)
            store(CHUNKS - 1, 0)
            sp.wait_ge(even_copied, CHUNKS + 1)
            sp.dma_start(table[CHUNKS * CW:VOCAB, :], w_out[0:TAIL, 1, 0, :]).then_inc(chunk_out[1], 16)

            for u in range(RING):
                sp.wait_ge(chunk_out[u], 16 * (ROUNDS + (u < 2)))
            sp.dma_start(w2s[:], W2.rearrange("e (c p) d -> p e c d", p=P)).then_inc(weights_in, 16)
            sp.dma_start(b2s[:], b2.rearrange("(a e) d -> a e d", a=1).to_broadcast([P, E, D])).then_inc(weights_in, 16)

            sp.wait_ge(tables_ready, 1)
            for e in range(E):
                at = sp.value_load(pad_i[0:1, e:e + 1], min_val=0, max_val=E * REGION - GR)
                sp.dma_start(xs[bass.ds(at, GR), :].rearrange("(p t) c -> p t c", t=GT), padding[:]).then_inc(padded, 16)
            sp.wait_ge(padded, 16 * E)
            for b in range(2):
                sp.wait_ge(scattered[b], 16 * NT * K * (B // 2))

            def load_group(j, b):
                start = sp.value_load(start_i[0:1, bass.ds(j, 1)], min_val=0, max_val=E * REGION - GR)
                e = sp.value_load(expert_i[0:1, bass.ds(j, 1)], min_val=0, max_val=E - 1)
                wait(sp, y_ready, j - XR + 1)
                sp.dma_start(rows[:, b], xs[bass.ds(start, GR), :].rearrange("(p t) c -> p t c", t=GT)).then_inc(group_in[b], 16)
                wait(sp, hidden_done, 2 * (j - XR + 1))
                sp.dma_start(w1c[:, b, :], W1[bass.ds(e, 1)].rearrange("a d f -> d (a f)")).then_inc(w1_in[b], 16)

            for b in range(XR):
                load_group(b, b)
            with sp.Fori(1, NJ // XR) as i:
                for b in range(XR):
                    load_group(i * XR + b, b)

            for b in range(XR):
                sp.wait_ge(y_out[b], 16 * GT * (NJ // XR))
            for c in range(4):
                for k in range(K):
                    r0 = k * N + c * QT * P
                    sp.dma_start(y_parts[:, k, c], ys[r0:r0 + QT * P, :].rearrange("(t p) d -> p t d", p=P)).then_inc(y_in[c], 16)
            flat = out.rearrange("b (t p) d -> p (b t) d", p=P)
            for c in range(4):
                sp.wait_ge(y_sum, c + 1)
                sp.dma_start(flat[:, c * QT:(c + 1) * QT, :], hall[:, c * QT:(c + 1) * QT, :]).then_inc(stored, 16)
            sp.wait_ge(stored, 16 * 4)

        @block.gpsimd
        def _(pool):
            nc.gpsimd.memset(ident[:], 0.0).then_inc(pool_init, 1)
            nc.gpsimd.memset(maskf[:], 0.0).then_inc(pool_init, 1)
            nc.gpsimd.memset(mean_w[:, 0:1], 1.0 / RQ)
            nc.gpsimd.memset(mean_w[:, 1:2], 1.0 / RKV)
            nc.gpsimd.memset(before[:], 1.0)
            nc.gpsimd.memset(onesb[:], 1.0)
            nc.gpsimd.memset(seen[:], 0.0)
            nc.gpsimd.memset(zero8[:], 0.0)
            nc.gpsimd.memset(padding[:], 0.0)
            nc.gpsimd.memset(row[:], 0.0)
            nc.gpsimd.iota(iota8[:], [[1, E]], base=0, channel_multiplier=0, allow_small_or_imprecise_dtypes=True)
            nc.gpsimd.iota(region8[:], [[REGION // P, E]], base=0, channel_multiplier=0, allow_small_or_imprecise_dtypes=True)
            nc.gpsimd.iota(iotaj[:], [[1, NJ]], base=0, channel_multiplier=0, allow_small_or_imprecise_dtypes=True)
            nc.gpsimd.iota(dest[:], [[P, NT], [N, K]], base=0, channel_multiplier=1, allow_small_or_imprecise_dtypes=True)
            nc.gpsimd.memset(neg_half[:], -0.5).then_inc(pool_init, 1)
            pool.wait_ge(pool_init, 3)
            nc.gpsimd.affine_select(out=ident[:], in_=ident[:], compare_op=ALU.not_equal, fill=1.0, base=0,
                                    pattern=[[-1, P]], channel_multiplier=1)
            nc.gpsimd.affine_select(out=before[:], in_=before[:], compare_op=ALU.is_ge, fill=0.0, base=-1,
                                    pattern=[[1, P]], channel_multiplier=-1)
            nc.gpsimd.iota(padding[:, :, DEST], [[P, GT]], base=K * N, channel_multiplier=1, allow_small_or_imprecise_dtypes=True)
            nc.gpsimd.affine_select(out=maskf[:], in_=maskf[:], compare_op=ALU.is_ge, fill=-1e30, base=0,
                                    pattern=[[-1, P]], channel_multiplier=1).then_inc(pool_init, 1)
            pool.wait_ge(ids_in, 16)
            for u in range(RING):
                pool.wait_ge(chunk_out[u], 16 * (ROUNDS + (u < 2)))

            def gather(s, b):
                nc.gpsimd.tensor_copy(ids_now[:, b, :], ids[:, bass.ds(s * NT, NT)]).then_inc(ids_copied, 1)
                pool.wait_ge(ids_copied, s + 1)
                stand_alone(pool, passed)
                for t in range(NT):
                    nc.gpsimd.indirect_dma_start(
                        out=gat[:, b, t, :], out_offset=None, in_=table[:, :],
                        in_offset=bass.IndirectOffsetOnAxis(ap=ids_now[:, b, t:t + 1], axis=0)).then_inc(rows_in[b], 16)

            E_STEPS = 10

            def embed_f(s, b, half):
                pool.wait_ge(rows_in[b], 16 * NT * (half + 1))
                wait(pool, mv_ready, s)
                wait(pool, x_ready, s)
                nc.gpsimd.tensor_tensor(out=f[:], in0=gat[:, b], in1=tokb[:].unsqueeze(1).to_broadcast([P, NT, D]),
                                        op=ALU.add).then_inc(f_ready, 1)

            def embed_x(s, b):
                k = [0]

                def link(ins):
                    k[0] += 1
                    ins.then_inc(e_pool, 1)
                    pool.wait_ge(e_pool, E_STEPS * s + k[0])
                    if k[0] in (2, 6, E_STEPS):
                        stand_alone(pool, passed)

                def tt(o, a, c, op):
                    link(nc.gpsimd.tensor_tensor(out=o, in0=a, in1=c, op=op))

                mean, var = mv[:, :, 0], mv[:, :, 1]
                e = [est[:, i, :] for i in range(10)]
                pool.wait_ge(mv_ready, s + 1)
                tt(e[0], mean, mean, ALU.mult)
                tt(e[0], e[0], var, ALU.add)
                link(nc.gpsimd.tensor_scalar(out=e[1], in0=e[0], scalar1=float(D), scalar2=1e-24, op0=ALU.mult, op1=ALU.max))
                tt(e[2], e[1], neg_half[:, 0:NT], ALU.pow)
                tt(e[3], e[2], e[2], ALU.mult)
                tt(e[3], e[3], var, ALU.mult)
                link(nc.gpsimd.tensor_scalar(out=e[4], in0=e[3], scalar1=1e-5, scalar2=None, op0=ALU.add))
                tt(e[5], e[4], neg_half[:, 0:NT], ALU.pow)
                tt(e[6], e[2], e[5], ALU.mult)
                tt(e[7], mean, e[6], ALU.mult)
                assert k[0] == E_STEPS
                nc.gpsimd.tensor_tensor(out=hall[:, bass.ds(s * NT, NT), :], in0=f[:],
                                        in1=e[2].unsqueeze(2).to_broadcast([P, NT, D]), op=ALU.mult)
                for t in range(NT):
                    last = nc.gpsimd.tensor_scalar(out=xn[:, b, t, :], in0=f[:, t, :], scalar1=e[6][:, t:t + 1],
                                                   scalar2=e[7][:, t:t + 1], op0=ALU.mult, op1=ALU.subtract)
                last.then_inc(x_ready, 1)

            P_STEPS = 6

            def project(s, b):
                k = [0]

                def link(ins):
                    k[0] += 1
                    ins.then_inc(p_pool, 1)
                    pool.wait_ge(p_pool, P_STEPS * s + k[0])

                pool.wait_ge(dve_stat, s + 1)
                nc.gpsimd.tensor_tensor(out=skv[:], in0=em[:, :, 1], in1=neg_half[:, 0:NT], op=ALU.pow).then_inc(skv_ready, 1)
                link(nc.gpsimd.tensor_scalar(out=epsq[:], in0=em[:, :, 0], scalar1=1e-6 * HD, scalar2=None, op0=ALU.mult))
                pool.wait_ge(dve_kv, s + 1)
                link(nc.gpsimd.tensor_tensor(out=kt[:, :, :, DN:HD], in0=krope_a[:], in1=krope_b[:], op=ALU.add))
                nc.gpsimd.tensor_tensor(out=ksq[:], in0=kt[:], in1=kt[:], op=ALU.mult).then_inc(ksq_ready, 1)
                for t in range(NT):
                    pool.wait_ge(dve_rope, NT * s + t + 1)
                    nc.gpsimd.tensor_tensor(out=qt[:, t].rearrange("p g k d -> p (g k) d")[:, :, DN:HD], in0=rope_a[:, t],
                                            in1=rope_b[:, t], op=ALU.add).then_inc(q_ready, 1)
                pool.wait_ge(kss_ready, s + 1)
                stand_alone(pool, passed)
                link(nc.gpsimd.tensor_scalar(out=rkv[:], in0=kss[:], scalar1=1.0 / HD, scalar2=1e-6, op0=ALU.mult, op1=ALU.add))
                link(nc.gpsimd.tensor_tensor(out=rk[:], in0=rkv[:], in1=neg_half[:, 0:NT * KVH], op=ALU.pow))
                kflat = kt[:].rearrange("p t k d -> p (t k) d")
                link(nc.gpsimd.tensor_tensor(out=kflat, in0=kflat, in1=rk[:].unsqueeze(2).to_broadcast([P, NT * KVH, HD]),
                                             op=ALU.mult))
                nc.gpsimd.tensor_tensor(out=kflat, in0=kflat, in1=khw[:].unsqueeze(1).to_broadcast([P, NT * KVH, HD]),
                                        op=ALU.mult).then_inc(k_ready, 1)
                pool.wait_ge(qss_ready, s + 1)
                link(nc.gpsimd.tensor_tensor(out=rqv[:], in0=qss[:], in1=epsq[:].unsqueeze(2).to_broadcast([P, NT, H]), op=ALU.add))
                assert k[0] == P_STEPS
                nc.gpsimd.tensor_tensor(out=rq[:, b].rearrange("p t g k -> p (t g k)"), in0=rqv[:].rearrange("p t h -> p (t h)"),
                                        in1=neg_half[:, 0:NT * H], op=ALU.pow).then_inc(rq_ready, 1)

            R_STEPS = 8

            def route_coefficients(r):
                k = [0]

                def link(ins):
                    k[0] += 1
                    ins.then_inc(r_pool, 1)
                    pool.wait_ge(r_pool, R_STEPS * r + k[0])

                def tt(o, a, c, op):
                    return nc.gpsimd.tensor_tensor(out=o, in0=a, in1=c, op=op)

                pool.wait_ge(mv2_ready, r + 1)
                stand_alone(pool, passed)
                mean, var = mv2[:, :, 0], mv2[:, :, 1]
                e = [rst[:, i, :] for i in range(10)]
                link(nc.gpsimd.tensor_scalar(out=e[0], in0=var, scalar1=1e-5, scalar2=None, op0=ALU.add))
                link(tt(e[1], e[0], neg_half[:, 0:NT], ALU.pow))
                link(tt(e[2], e[1], e[1], ALU.mult))
                link(tt(e[2], e[2], var, ALU.mult))
                stand_alone(pool, passed)
                link(nc.gpsimd.tensor_scalar(out=e[3], in0=e[2], scalar1=1e-5, scalar2=None, op0=ALU.add))
                link(tt(e[4], e[3], neg_half[:, 0:NT], ALU.pow))
                link(tt(e[5], e[4], e[1], ALU.mult))
                tt(e[6], mean, e[5], ALU.mult)
                link(tt(e[7], mean, e[1], ALU.mult))
                stand_alone(pool, passed)
                assert k[0] == R_STEPS
                nc.gpsimd.tensor_scalar(out=e[8], in0=e[1], scalar1=1.0, scalar2=None, op0=ALU.add).then_inc(coef_ready, 1)

            def dispatch(r, b, half):
                pool.wait_ge(hh_ready, r + 1)
                stand_alone(pool, passed)
                nc.gpsimd.tensor_copy(row[:, b, :, 1, 0:D], row[:, b, :, 0, 0:D])
                nc.gpsimd.tensor_copy(row[:, b, :, :, DEST], dest[:]).then_inc(row_full, 1)
                pool.wait_ge(row_full, 2 * r + 1)
                stand_alone(pool, passed)
                nc.gpsimd.tensor_scalar(out=dest[:], in0=dest[:], scalar1=float(T), scalar2=None, op0=ALU.add).then_inc(row_full, 1)
                pool.wait_ge(row_full, 2 * r + 2)
                pool.wait_ge(slot_ready, r + 1)
                stand_alone(pool, passed)
                for t in range(NT):
                    for k in range(K):
                        i = t * K + k
                        nc.gpsimd.indirect_dma_start(
                            out=xs[:, :], out_offset=bass.IndirectOffsetOnAxis(ap=slot[:, b, i:i + 1], axis=0),
                            in_=row[:, b, t, k, :], in_offset=None).then_inc(scattered[b], 16)

            def body(s, b, half):
                if not isinstance(s, int) or s > 0:
                    route_coefficients(s - 1)
                if not isinstance(s, int) or s + 3 < B:
                    gather(s + 3, 1 - b)
                if not isinstance(s, int) or s + 2 < B:
                    embed_f(s + 2, b, half + 1)
                if not isinstance(s, int) or s + 1 < B:
                    project(s + 1, 1 - b)
                if not isinstance(s, int) or s + 2 < B:
                    embed_x(s + 2, b)
                if not isinstance(s, int) or s > 0:
                    dispatch(s - 1, 1 - b, half)

            gather(0, 0)
            gather(1, 1)
            pool.wait_ge(consts_in, 16 * SMALL)
            embed_f(0, 0, 0)
            embed_x(0, 0)
            gather(2, 0)
            embed_f(1, 1, 0)
            embed_x(1, 1)
            project(0, 0)
            for s in (0, 1, 2):
                body(s, s % 2, s // 2)
            with pool.Fori(1, 6) as i:
                body(i * 2 + 1, 1, i)
                body(i * 2 + 2, 0, i + 1)
            for s in (13, 14, 15):
                body(s, s % 2, s // 2)
            route_coefficients(B - 1)
            dispatch(B - 1, 1, 0)

            def scatter_y(j, b):
                pool.wait_ge(y_ready, j + 1)
                stand_alone(pool, passed)
                for t in range(GT):
                    nc.gpsimd.indirect_dma_start(
                        out=ys[:, :], out_offset=bass.IndirectOffsetOnAxis(ap=where[:, b, t:t + 1], axis=0), in_=yb[:, b, t, :],
                        in_offset=None, bounds_check=K * N - 1, oob_is_err=False).then_inc(y_out[b], 16)

            with pool.Fori(0, NJ // XR) as i:
                for b in range(XR):
                    scatter_y(i * XR + b, b)

        @block.scalar
        def _(act):
            def small(dst, src):
                act.dma_start(dst, src).then_inc(consts_in, 16)

            def row_(a):
                return a.rearrange("(a n) -> a n", a=1)

            def col(a):
                return a.rearrange("(n a) -> n a", a=1)

            with nc.allow_non_contiguous_dma(reason="small tables"):
                act.dma_start(ids[:, :].rearrange("p (b t) -> p b t", b=B), x.rearrange("b (t p) -> p b t", p=P)).then_inc(ids_in, 16)
                small(tokb[:], row_(tok_b).to_broadcast([P, D]))
                small(cossin[:], rope)
                small(wdq[:], W_DQ)
                small(wdkv[:], W_DKV)
                small(wkr[:], W_KR)
                for a in range(KVH):
                    small(wq_raw[:, :, a, 0:DN], W_UQ.rearrange("c (a j d) -> c a j d", a=KVH, j=G)[:, a])
                    small(wq_raw[:, :, a, DN:HD], W_QR.rearrange("c (a j d) -> c a j d", a=KVH, j=G)[:, a])
                    small(wvr[:, :, a, :], W_VR.rearrange("c (a j d) -> c a j d", a=KVH, j=G)[:, a])
                    small(wo[HD * a:HD * a + HD, :, :], W_O.rearrange("(a j d) n -> a d j n", a=KVH, j=G)[a])
                small(wkv_raw[:, 0:KVH * DN], W_UK)
                small(wkv_raw[:, KVH * DN:], W_UV)
                small(qln[:], col(q_ln_w))
                small(kvln[:], col(kv_ln_w))
                small(lng[:], col(ln_g))
                small(lnb[:], col(ln_b))
                small(br[:], row_(b_r).to_broadcast([P, E]))
                small(wrT[:], w_r.rearrange("e d -> d e"))
                small(b1s[:].rearrange("p e c -> p (e c)"), b1.rearrange("e (c p) -> p (e c)", p=P))
                small(hw2[:, 0, :], row_(qh_w).to_broadcast([P, HD]))
                small(hw2[:, 1, :], row_(kh_w).to_broadcast([P, HD]))

            def copy(dst, src):
                return nc.scalar.activation(dst, src, ACT.Copy)

            def table_chunk(n, u, i):
                act.wait_ge(turned, 2 * n + 1)
                wait(act, chunk_out[u], 16 * i)
                copy(w_out[:, u, 0:4, :].rearrange("p j d -> p (j d)"), banks[2 * (u % 4)][:, :]).then_inc(even_copied, 1)

            for u in range(RING):
                table_chunk(u, u, 0)
            with act.Fori(1, ROUNDS) as i:
                for u in range(RING):
                    table_chunk(i * RING + u, u, i)
            table_chunk(CHUNKS - 1, 0, ROUNDS)
            act.wait_ge(turned, 2 * CHUNKS + 1)
            wait(act, chunk_out[1], 16 * ROUNDS)
            copy(w_out[0:TAIL, 1, 0, :], banks[2][0:TAIL, 0:D]).then_inc(even_copied, 1)

            act.wait_ge(setup_pe, 1)
            copy(wvrT[:].rearrange("p j d -> p (j d)"), banks[0][:, :]).then_inc(setup_act, 1)
            act.wait_ge(setup_pe, 2)
            copy(wvo[:], banks[1][:, 0:D]).then_inc(setup_act, 1)

            def p_xT(s, b, routed=False):
                act.wait_ge(pe_xT, s + 1)
                if routed:
                    act.wait_ge(pe_h, s - 1)
                wait(act, pe_wo, s - 1)
                copy(xT[:, b, :], M0[:, 0:T]).then_inc(act_xT, 1)

            def p_sq(s, b):
                act.wait_ge(dve_c, s + 1)
                nc.scalar.activation(sqc[0:RQ, 0, :], cqT[:], ACT.Square)
                nc.scalar.activation(sqc[:, 1, :], ckvT[:], ACT.Square).then_inc(act_sq, 1)

            def p_q(s, b, t):
                M = (M1, M0)[t]
                act.wait_ge(pe_q, NT * s + t + 1)
                wait(act, qss_ready, s)
                nc.scalar.activation(qsq[:, t].rearrange("p h d -> p (h d)"), M[:, :], ACT.Square)
                copy(qt[:, t].rearrange("p g k d -> p (g k) d")[:, :, 0:DN],
                     M[:, :].rearrange("p (h d) -> p h d", d=HD)[:, :, 0:DN]).then_inc(act_q, 1)

            def p_qT(s, b, t):
                act.wait_ge(pe_qT, NT * s + t + 1)
                copy(qT[:, b, t].rearrange("p j q -> p (j q)"), (M1, M0)[t][:, :]).then_inc(act_qT, 1)

            def p_kT(s, b):
                act.wait_ge(pe_kT, s + 1)
                copy(kT[:, b, :], M1[:, 0:T]).then_inc(act_kT, 1)

            def exps(s, b, u):
                t, kv, j0, n = UNITS[u]
                act.wait_ge(bias_ready, NU * s + u + 1)
                before = (u - 2) % NU
                bank, use = t_use("p", before)
                wait(act, t_full[bank], 4 * (s - (u < 2)) + use + 1)
                w = P * (t + 1)
                for c in range(n):
                    last = nc.scalar.activation(pm[:, u % 2, c * w:(c + 1) * w], S[u % 3][:, c * w:(c + 1) * w], ACT.Exp,
                                                bias=nbias[:, u, c:c + 1], scale=rq[:, b, t, j0 + c, kv:kv + 1],
                                                accum_out=rsum[:, t, j0 + c, kv:kv + 1])
                last.then_inc(exped, 1)

            def pt_copy(s, b, u):
                pt_evacuate(act, copy, s, u)

            def r_copy(s, b, t):
                bank, use = t_use("r", t)
                act.wait_ge(t_full[bank], 4 * s + use + 1)
                wait(act, on_ready[t], s)
                copy(rb[:, t, :], TB[bank][:, :]).then_inc(t_free[bank], 1)

            def route_h(r):
                act.wait_ge(pe_h, r + 1)
                nc.scalar.activation(hfT[:], M0[:, T:2 * T], ACT.Identity, bias=lnb[:, 0:1], scale=lng[:, 0:1]).then_inc(act_h, 1)

            def route_e(r):
                act.wait_ge(dlog_ready, r + 1)
                nc.scalar.activation(eg[:], dlog[:], ACT.Exp).then_inc(eg_ready, 1)

            def body(s, b):
                more = not isinstance(s, int) or s + 1 < B
                routed = not isinstance(s, int) or s > 0
                s1, b1_ = s + 1, 1 - b
                exps(s, b, 0)
                exps(s, b, 1)
                if more:
                    p_xT(s1, b1_, routed)
                if routed:
                    route_h(s - 1)
                pt_copy(s, b, 1)
                exps(s, b, 2)
                if more:
                    p_sq(s1, b1_)
                r_copy(s, b, 0)
                exps(s, b, 3)
                if more:
                    p_q(s1, b1_, 0)
                pt_copy(s, b, 3)
                exps(s, b, 4)
                if more:
                    p_q(s1, b1_, 1)
                exps(s, b, 5)
                pt_copy(s, b, 5)
                if more:
                    p_qT(s1, b1_, 0)
                r_copy(s, b, 1)
                if routed:
                    route_e(s - 1)
                if more:
                    p_qT(s1, b1_, 1)
                    p_kT(s1, b1_)

            p_xT(0, 0)
            p_sq(0, 0)
            p_q(0, 0, 0)
            p_q(0, 0, 1)
            p_qT(0, 0, 0)
            p_qT(0, 0, 1)
            p_kT(0, 0)
            for s in (0, 1, 2):
                body(s, s % 2)
            with act.Fori(1, 6) as i:
                body(i * 2 + 1, 1)
                body(i * 2 + 2, 0)
            for s in (13, 14, 15):
                body(s, s % 2)
            route_h(B - 1)
            route_e(B - 1)

            def gelu(j, b):
                act.wait_ge(biases_ready, j + 1)
                wait(act, y_done, j - 1)
                for half in range(2):
                    act.wait_ge(hidden_done, 2 * j + half + 1)
                    for c in range(2 * half, 2 * half + 2):
                        last = nc.scalar.activation(hid[:, b % 2, c, :], HID[b % 2][half][:, (c % 2) * GR:(c % 2 + 1) * GR],
                                                    ACT.Gelu, bias=b1c[:, b, c:c + 1])
                    last.then_inc(hid_ready, 1)

            for b in range(XR):
                gelu(b, b)
            with act.Fori(1, NJ // XR) as i:
                for b in range(XR):
                    gelu(i * XR + b, b)

        @block.vector
        def _(dve):
            dve.wait_ge(pool_init, 4)
            nc.vector.tensor_copy(identb[:], ident[:])
            nc.vector.tensor_copy(beforeb[:], before[:])
            nc.vector.tensor_scalar(region8[:], region8[:], float(P), None, ALU.mult)
            for j in range(4):
                nc.vector.tensor_copy(masks[:, 0, j * P:(j + 1) * P], maskf[:])
            for j in range(2):
                nc.vector.memset(masks[:, 1, 2 * j * P:(2 * j + 1) * P], 0.0)
                nc.vector.tensor_copy(masks[:, 1, (2 * j + 1) * P:(2 * j + 2) * P], maskf[:])
            dve.wait_ge(consts_in, 16 * SMALL)
            nc.vector.tensor_scalar(wq[:], wq_raw[:].rearrange("p g k d -> p (g k d)"), qln[:, 0:1], None, ALU.mult)
            nc.vector.tensor_scalar(wkv[:], wkv_raw[:], kvln[:, 0:1], None, ALU.mult)
            nc.vector.tensor_tensor(khw[:], hw2[:, 0, :], hw2[:, 1, :], ALU.mult).then_inc(dve_init, 1)

            def table_chunk(n, u, i):
                dve.wait_ge(turned, 2 * n + 2)
                wait(dve, chunk_out[u], 16 * i)
                nc.vector.tensor_copy(w_out[:, u, 4:8, :].rearrange("p j d -> p (j d)"), banks[2 * (u % 4) + 1][:, :]).then_inc(odd_copied, 1)

            for u in range(RING):
                table_chunk(u, u, 0)
            with dve.Fori(1, ROUNDS) as i:
                for u in range(RING):
                    table_chunk(i * RING + u, u, i)
            table_chunk(CHUNKS - 1, 0, ROUNDS)

            def embed(s):
                dve.wait_ge(f_ready, s + 1)
                for t in range(NT):
                    last = nc.vector.bn_stats(bst[:, t, :], f[:, t, :])
                last.then_inc(e_dve, 1)
                dve.wait_ge(e_dve, s + 1)
                wait(dve, x_ready, s)
                stand_alone(dve, passed)
                for t in range(NT):
                    last = nc.vector.bn_aggr(mv[:, t, :], bst[:, t, :])
                last.then_inc(mv_ready, 1)

            def copy(dst, src):
                return nc.vector.tensor_copy(dst, src)

            def p_c(s, b):
                dve.wait_ge(pe_c, s + 1)
                nc.vector.tensor_copy(cqT[:], M1[0:RQ, 0:T])
                nc.vector.tensor_copy(ckvT[:], M1[:, T:2 * T]).then_inc(dve_c, 1)

            def p_stat(s, b, routed):
                dve.wait_ge(pe_stat, s + 1)
                if routed:
                    dve.wait_ge(pe_logits, s - 1)
                wait(dve, rq_ready, s)
                nc.vector.tensor_scalar(em[:].rearrange("p t c -> p (t c)"), M1[:, 0:2 * NT], 1e-6, None, ALU.add).then_inc(dve_stat, 1)

            def rotate(oa, ob, src, t_cos, t_sin):
                h = DR // 2
                nc.vector.tensor_tensor(oa, src, t_cos, ALU.mult)
                nc.vector.tensor_tensor(ob[..., 0:h], src[..., h:DR], t_sin[..., 0:h], ALU.mult)
                return nc.vector.tensor_tensor(ob[..., h:DR], src[..., 0:h], t_sin[..., h:DR], ALU.mult)

            def p_kv(s, b):
                dve.wait_ge(pe_kv, s + 1)
                wait(dve, k_ready, s)
                m = M0[:, :].rearrange("p (t c) -> p t c", t=NT)
                shape = [P, NT, KVH, DR]
                rotate(krope_a[:], krope_b[:], m[:, :, 192:256].rearrange("p t (k d) -> p t k d", k=KVH),
                       cossin[:, 0].unsqueeze(2).to_broadcast(shape), cossin[:, 1].unsqueeze(2).to_broadcast(shape))
                dve.wait_ge(skv_ready, s + 1)
                nc.vector.tensor_tensor(kt[:, :, :, 0:DN], m[:, :, 0:64].rearrange("p t (k d) -> p t k d", k=KVH),
                                        skv[:].unsqueeze(2).unsqueeze(3).to_broadcast(shape), ALU.mult)
                nc.vector.tensor_tensor(v[:, b], m[:, :, 64:192], skv[:].unsqueeze(2).to_broadcast([P, NT, KVH * HD]),
                                        ALU.mult).then_inc(dve_kv, 1)

            def p_rope(s, b, t):
                dve.wait_ge(act_q, NT * s + t + 1)
                wait(dve, q_ready, NT * s - NT + t + 1)
                src = (M1, M0)[t][:, :].rearrange("p (h d) -> p h d", d=HD)[:, :, DN:HD]
                shape = [P, H, DR]
                rotate(rope_a[:, t], rope_b[:, t], src, cossin[:, 0, t].unsqueeze(1).to_broadcast(shape),
                       cossin[:, 1, t].unsqueeze(1).to_broadcast(shape)).then_inc(dve_rope, 1)

            def p_kss(s):
                dve.wait_ge(ksq_ready, s + 1)
                nc.vector.reduce_sum(kss[:], ksq[:].rearrange("p t k d -> p (t k) d"), AX.X).then_inc(kss_ready, 1)

            def p_qss(s):
                dve.wait_ge(act_q, NT * s + NT)
                nc.vector.reduce_sum(qss[:].rearrange("p t h -> p (t h)"), qsq[:].rearrange("p t h d -> p (t h) d"), AX.X).then_inc(qss_ready, 1)

            def bias(s, b, u):
                t, kv, j0, n = UNITS[u]
                dve.wait_ge(scored, NU * s + u + 1)
                nc.vector.tensor_reduce(negmax[:, u, 0:n], S[u % 3][:, :].rearrange("p (c k) -> p c k", c=n), AX.X, ALU.max,
                                        negate=True).then_inc(max_done, 1)
                dve.wait_ge(max_done, NU * s + u + 1)
                if u == 0:
                    dve.wait_ge(rq_ready, s + 1)
                nc.vector.tensor_tensor(nbias[:, u, 0:n], negmax[:, u, 0:n], rq[:, b, t, j0:j0 + n, kv], ALU.mult).then_inc(bias_ready, 1)

            def recip(s, t):
                dve.wait_ge(exped, NU * s + (2, NU)[t])
                nc.vector.reciprocal(rinv[:, t].rearrange("p g k -> p (g k)"), rsum[:, t].rearrange("p g k -> p (g k)")).then_inc(rinv_done, 1)
                dve.wait_ge(rinv_done, NT * s + t + 1)
                nc.vector.tensor_copy(rwide[:, t].rearrange("p g (k d) -> p (g k) d", k=KVH),
                                      rinv[:, t].rearrange("p g k -> p (g k)").unsqueeze(2).to_broadcast([P, H, HD])).then_inc(rinv_ready, 1)

            def normalise(s, t):
                bank, use = t_use("r", t)
                dve.wait_ge(pv_done[t], s + 1)
                dve.wait_ge(t_free[bank], 4 * s + use + 1)
                wait(dve, pe_wo, s)
                nc.vector.tensor_tensor(on[:, t].rearrange("p j q -> p (j q)"), O[:, :], rb[:, t, :], ALU.mult).then_inc(on_ready[t], 1)

            def residual(s):
                dve.wait_ge(pe_wo, s + 1)
                h = hall[:, bass.ds(s * NT, NT), :]
                nc.vector.tensor_tensor(h, O[:, 0:NT * D].rearrange("p (t d) -> p t d", t=NT), h, ALU.add).then_inc(h_added, 1)

            def route_stats(r):
                dve.wait_ge(h_added, r + 1)
                stand_alone(dve, passed)
                for t in range(NT):
                    last = nc.vector.bn_stats(bst2[:, t, :], hall[:, bass.ds(r * NT + t, 1), :].rearrange("p a d -> p (a d)"))
                last.then_inc(r_stats, 1)
                dve.wait_ge(r_stats, r + 1)
                stand_alone(dve, passed)
                for t in range(NT):
                    last = nc.vector.bn_aggr(mv2[:, t, :], bst2[:, t, :])
                last.then_inc(mv2_ready, 1)

            def route_hh(r, b, half):
                dve.wait_ge(coef_ready, r + 1)
                wait(dve, scattered[b], 16 * NT * K * half)
                h = [hall[:, bass.ds(r * NT + t, 1), :].rearrange("p a d -> p (a d)") for t in range(NT)]
                for t in range(NT):
                    last = nc.vector.tensor_scalar(row[:, b, t, 0, 0:D], h[t], rst[:, 5, t:t + 1], rst[:, 6, t:t + 1],
                                                   ALU.mult, ALU.subtract)
                last.then_inc(hh_ready, 1)
                for t in range(NT):
                    last = nc.vector.tensor_scalar(h[t], h[t], rst[:, 8, t:t + 1], rst[:, 7, t:t + 1], ALU.mult, ALU.subtract)
                last.then_inc(base_ready, 1)

            TOP_STEPS = 4

            def route_logits(r):
                dve.wait_ge(pe_logits, r + 1)
                nc.vector.tensor_tensor(lg[:], M1[:, 4:4 + NT * E].rearrange("p (t e) -> p t e", t=NT),
                                        br[:].unsqueeze(1).to_broadcast([P, NT, E]), ALU.add).then_inc(logits_copied, 1)

            def route_top(r):
                k = [0]

                def link(ins):
                    k[0] += 1
                    ins.then_inc(r_dve, 1)
                    dve.wait_ge(r_dve, TOP_STEPS * r + k[0])

                dve.wait_ge(logits_copied, r + 1)
                stand_alone(dve, passed)
                nc.vector.max(mx8[:, 0], lg[:, 0])
                link(nc.vector.max(mx8[:, 1], lg[:, 1]))
                stand_alone(dve, passed)
                nc.vector.max_index(ix8[:, 0], mx8[:, 0], lg[:, 0])
                link(nc.vector.max_index(ix8[:, 1], mx8[:, 1], lg[:, 1]))
                nc.vector.tensor_tensor(dlog[:], mx8[:, :, 1], mx8[:, :, 0], ALU.subtract).then_inc(dlog_ready, 1)
                link(nc.vector.tensor_copy(ixf[:], ix8[:, :, 0:K]))
                shape = [P, NT * K, E]
                link(nc.vector.tensor_tensor(chosen[:].rearrange("p t k e -> p (t k) e"),
                                             ixf[:].rearrange("p t k -> p (t k)").unsqueeze(2).to_broadcast(shape),
                                             iota8[:].unsqueeze(1).to_broadcast(shape), ALU.is_equal))
                nc.vector.tensor_tensor(both[:], chosen[:, :, 0], chosen[:, :, 1], ALU.add).then_inc(both_ready, 1)
                assert k[0] == TOP_STEPS

            GATE_STEPS = 2

            def route_gates(r, b):
                dve.wait_ge(eg_ready, r + 1)
                nc.vector.tensor_scalar(eg1[:], eg[:], 1.0, None, ALU.add).then_inc(g_dve, 1)
                dve.wait_ge(g_dve, GATE_STEPS * r + 1)
                nc.vector.reciprocal(row[:, b, :, 0, GATE], eg1[:]).then_inc(g_dve, 1)
                dve.wait_ge(g_dve, GATE_STEPS * r + 2)
                nc.vector.tensor_tensor(row[:, b, :, 1, GATE], eg[:], row[:, b, :, 0, GATE], ALU.mult)

            SLOT_STEPS = 4

            def route_slots(r, b):
                k = [0]

                def link(ins):
                    k[0] += 1
                    ins.then_inc(c_dve, 1)
                    dve.wait_ge(c_dve, SLOT_STEPS * r + k[0])

                dve.wait_ge(pe_rank, r + 1)
                nc.vector.tensor_tensor(pos[:], M1[:, T:T + NT * E].rearrange("p (t e) -> p t e", t=NT),
                                        region8[:].unsqueeze(1).to_broadcast([P, NT, E]), ALU.add).then_inc(rank_copied, 1)
                dve.wait_ge(rank_copied, r + 1)
                link(nc.vector.tensor_tensor(posk[:], chosen[:], pos[:].unsqueeze(2).to_broadcast([P, NT, K, E]), ALU.mult))
                link(nc.vector.reduce_sum(slotf[:], posk[:].rearrange("p t k e -> p (t k) e"), AX.X))
                nc.vector.tensor_copy(slot[:, b], slotf[:]).then_inc(slot_ready, 1)
                for t in range(NT):
                    link(nc.vector.tensor_tensor(seen[:], seen[:], both[:, t], ALU.add))
                assert k[0] == SLOT_STEPS

            def body(s, b, half):
                more = not isinstance(s, int) or s + 1 < B
                routed = not isinstance(s, int) or s > 0
                more2 = not isinstance(s, int) or s + 2 < B
                s1, b1_ = s + 1, 1 - b
                bias(s, b, 0)
                bias(s, b, 1)
                if routed:
                    route_hh(s - 1, 1 - b, half)
                pt_evacuate(dve, copy, s, 0)
                bias(s, b, 2)
                recip(s, 0)
                if more:
                    p_c(s1, b1_)
                if more2:
                    embed(s + 2)
                bias(s, b, 3)
                if more:
                    p_stat(s1, b1_, routed)
                if routed:
                    route_logits(s - 1)
                pt_evacuate(dve, copy, s, 2)
                normalise(s, 0)
                bias(s, b, 4)
                if more:
                    p_kv(s1, b1_)
                    p_rope(s1, b1_, 0)
                bias(s, b, 5)
                if more:
                    p_kss(s1)
                    p_rope(s1, b1_, 1)
                pt_evacuate(dve, copy, s, 4)
                if routed:
                    route_top(s - 1)
                if more:
                    p_qss(s1)
                recip(s, 1)
                normalise(s, 1)
                residual(s)
                route_stats(s)
                if routed:
                    route_gates(s - 1, 1 - b)
                    route_slots(s - 1, 1 - b)

            embed(0)
            embed(1)
            p_c(0, 0)
            p_stat(0, 0, False)
            p_kv(0, 0)
            p_rope(0, 0, 0)
            p_kss(0)
            p_rope(0, 0, 1)
            p_qss(0)
            for s in (0, 1, 2):
                body(s, s % 2, (s - 1) // 2)
            with dve.Fori(1, 6) as i:
                body(i * 2 + 1, 1, i)
                body(i * 2 + 2, 0, i)
            for s in (13, 14, 15):
                body(s, s % 2, (s - 1) // 2)
            r = B - 1
            route_hh(r, 1, r // 2)
            route_logits(r)
            route_top(r)
            route_gates(r, 1)
            route_slots(r, 1)

            k = [0]

            def then(ins):
                k[0] += 1
                ins.then_inc(t_dve, 1)
                dve.wait_ge(t_dve, k[0])

            dve.wait_ge(pe_count, 1)
            je_shape = [1, NJ, E]
            region, experts = region8[0:1, :], iota8[0:1, :]
            then(nc.vector.tensor_copy(cnt[:], M1[0:1, 2 * T - E:2 * T]))
            then(nc.vector.tensor_scalar(cnti[:], cnt[:], float(GR - 1), None, ALU.add))
            then(nc.vector.tensor_scalar(cntt[:], cnti[:], GR.bit_length() - 1, None, ALU.logical_shift_right))
            then(nc.vector.tensor_copy(ntile[:], cntt[:]))
            then(nc.vector.tensor_tensor_scan(tend[:], ntile[:], zero8[:], 0.0, ALU.add, ALU.add))
            then(nc.vector.tensor_tensor(tbase[:], tend[:], ntile[:], ALU.subtract))
            then(nc.vector.scalar_tensor_tensor(tbase[:], tbase[:], -float(GR), region, ALU.mult, ALU.add))
            then(nc.vector.tensor_tensor(je[:], iotaj[:].unsqueeze(2).to_broadcast(je_shape),
                                         tend[:].unsqueeze(1).to_broadcast(je_shape), ALU.is_ge))
            then(nc.vector.reduce_sum(jexp[:], je[:], AX.X))
            then(nc.vector.tensor_tensor(je[:], jexp[:].unsqueeze(2).to_broadcast(je_shape),
                                         experts.unsqueeze(1).to_broadcast(je_shape), ALU.is_equal))
            then(nc.vector.tensor_tensor(je[:], je[:], tbase[:].unsqueeze(1).to_broadcast(je_shape), ALU.mult))
            then(nc.vector.reduce_sum(jstart[:], je[:], AX.X))
            then(nc.vector.scalar_tensor_tensor(jstart[:], iotaj[:], float(GR), jstart[:], ALU.mult, ALU.add))
            then(nc.vector.tensor_scalar(jvalid[:], jexp[:], float(E), None, ALU.is_lt))
            then(nc.vector.tensor_scalar(jstart[:], jstart[:], cnt[:, 0:1], None, ALU.subtract))
            then(nc.vector.tensor_tensor(jstart[:], jstart[:], jvalid[:], ALU.mult))
            then(nc.vector.tensor_scalar(start_i[:], jstart[:], cnt[:, 0:1], None, ALU.add))
            then(nc.vector.tensor_tensor(expert_i[:], jexp[:], jvalid[:], ALU.mult))
            then(nc.vector.tensor_tensor(padrow[:], region, cnt[:], ALU.add))
            nc.vector.tensor_copy(pad_i[:], padrow[:]).then_inc(tables_ready, 1)

            def take_biases(j, b):
                e = dve.value_load(expert_i[0:1, bass.ds(j, 1)], min_val=0, max_val=E - 1)
                wait(dve, hid_ready, 2 * (j - XR + 1))
                nc.vector.tensor_copy(b2c[:, b, :], b2s[:, bass.ds(e, 1), :].rearrange("p a f -> p (a f)"))
                nc.vector.tensor_copy(b1c[:, b, :], b1s[:, bass.ds(e, 1), :].rearrange("p a f -> p (a f)")).then_inc(biases_ready, 1)

            def take_rows(j, b, turn):
                dve.wait_ge(x_turned, j + 1)
                wait(dve, hidden_done, 2 * (j - 1))
                nc.vector.tensor_scalar(hT[:, b % 2, :], XT[b % 2][:, 0:GR], lng[:, 0:1], lnb[:, 0:1], ALU.mult, ALU.add).then_inc(hT_ready, 1)
                wait(dve, y_out[b], 16 * GT * turn)
                nc.vector.tensor_copy(where[:, b, :], rows[:, b, :, DEST])

            def give_y(j, b):
                dve.wait_ge(y_done, j + 1)
                nc.vector.tensor_tensor(yt[:, b % 2], Y[b % 2][:, 0:GT * D].rearrange("p (t d) -> p t d", t=GT),
                                        b2c[:, b].unsqueeze(1).to_broadcast([P, GT, D]), ALU.add).then_inc(y_biased, 1)
                dve.wait_ge(y_biased, j + 1)
                for t in range(GT):
                    last = nc.vector.tensor_scalar(yb[:, b, t, :], yt[:, b % 2, t, :], rows[:, b, t, GATE:GATE + 1], None, ALU.mult)
                last.then_inc(y_ready, 1)

            def expert_steps(i):
                for b in range(XR):
                    ahead, b2_ = i * XR + b + 2, (b + 2) % XR
                    if not isinstance(i, int) or ahead < NJ:
                        take_rows(ahead, b2_, i + (b + 2) // XR)
                        take_biases(ahead, b2_)
                    give_y(i * XR + b, b)

            dve.wait_ge(weights_in, 32)
            for b in range(2):
                take_rows(b, b, 0)
                take_biases(b, b)
            expert_steps(0)
            with dve.Fori(1, NJ // XR - 1) as i:
                expert_steps(i)
            expert_steps(NJ // XR - 1)

            dve.wait_ge(base_ready, B)
            for c in range(4):
                h = hall[:, c * QT:(c + 1) * QT, :]
                dve.wait_ge(y_in[c], 32)
                nc.vector.tensor_tensor(h, h, y_parts[:, 0, c], ALU.add).then_inc(y_add, 1)
                dve.wait_ge(y_add, c + 1)
                nc.vector.tensor_tensor(h, h, y_parts[:, 1, c], ALU.add).then_inc(y_sum, 1)

        @block.tensor
        def _(pe):
            mm = nc.tensor.matmul
            pe.wait_ge(pool_init, 4)

            def table_chunk(n, u, i):
                pe.wait_ge(chunk_in[u], 16 * (i + 1))
                wait(pe, even_copied, n - 3)
                wait(pe, odd_copied, n - 3)
                w = w_in[:, u, :].rearrange("p (c j) -> p j c", j=CJ)
                for j in range(CJ):
                    last = nc.tensor.transpose(banks[2 * (u % 4) + j // 4][:, (j % 4) * P:(j % 4 + 1) * P], w[:, j], ident[:])
                    if j % 4 == 3:
                        last.then_inc(turned, 1)

            for u in range(RING):
                table_chunk(u, u, 0)
            with pe.Fori(1, ROUNDS) as i:
                for u in range(RING):
                    table_chunk(i * RING + u, u, i)
            table_chunk(CHUNKS - 1, 0, ROUNDS)
            pe.wait_ge(chunk_in[1], 16 * (ROUNDS + 1))
            pe.wait_ge(even_copied, CHUNKS - 3)
            pe.wait_ge(odd_copied, CHUNKS - 3)
            nc.tensor.transpose(banks[2][0:TAIL, 0:D], w_in[:, 1, 0:TAIL], ident[:]).then_inc(turned, 1)

            pe.wait_ge(even_copied, CHUNKS + 1)
            pe.wait_ge(odd_copied, CHUNKS)
            pe.wait_ge(consts_in, 16 * SMALL)
            pe.wait_ge(dve_init, 1)
            for j in range(G):
                w = wvr[:, j].rearrange("p a d -> p (a d)")
                last = nc.tensor.transpose(banks[0][:, j * P:(j + 1) * P], w, ident[:])
            last.then_inc(setup_pe, 1)
            pe.wait_ge(setup_act, 1)
            for j in range(G):
                last = mm(banks[1][:, 0:D], wvrT[:, j, :], wo[:, j, :], start=(j == 0), stop=(j == G - 1))
            last.then_inc(setup_pe, 1)
            pe.wait_ge(setup_act, 2)

            def p_a(s, b):
                pe.wait_ge(x_ready, s + 1)
                wait(pe, act_qT, NT * s)
                for t in range(NT):
                    last = nc.tensor.transpose(M0[:, t * P:(t + 1) * P], xn[:, b, t, :], ident[:])
                last.then_inc(pe_xT, 1)

            def p_b(s, b):
                pe.wait_ge(act_xT, s + 1)
                wait(pe, act_kT, s)
                wait(pe, rank_copied, s - 2)
                mm(M1[0:RQ, 0:T], wdq[:], xT[:, b, :], start=True, stop=True)
                mm(M1[:, T:2 * T], wdkv[:], xT[:, b, :], start=True, stop=True).then_inc(pe_c, 1)

            def p_stats(s, b):
                pe.wait_ge(act_sq, s + 1)
                pe.wait_ge(dve_c, s + 1)
                for t in range(NT):
                    tok = slice(t * P, (t + 1) * P)
                    mm(M1[:, 2 * t:2 * t + 1], sqc[0:RQ, 0, tok], mean_w[0:RQ, 0:1], start=True, stop=True)
                    last = mm(M1[:, 2 * t + 1:2 * t + 2], sqc[:, 1, tok], mean_w[:, 1:2], start=True, stop=True)
                last.then_inc(pe_stat, 1)

            def route_turn(r, b):
                pe.wait_ge(hh_ready, r + 1)
                wait(pe, act_h, r)
                wait(pe, act_qT, min(NT * (r + 2), NT * B) if isinstance(r, int) else NT * (r + 2))
                for t in range(NT):
                    last = nc.tensor.transpose(M0[:, T + t * P:T + (t + 1) * P], row[:, b, t, 0, 0:D], ident[:])
                last.then_inc(pe_h, 1)

            def route_logits(r):
                pe.wait_ge(act_h, r + 1)
                wait(pe, rank_copied, r)
                for t in range(NT):
                    last = mm(M1[:, 4 + E * t:4 + E * (t + 1)], hfT[:, t * P:(t + 1) * P], wrT[:], start=True, stop=True)
                last.then_inc(pe_logits, 1)

            def route_rank(r):
                pe.wait_ge(both_ready, r + 1)
                pe.wait_ge(act_kT, min(r + 3, B) if isinstance(r, int) else r + 3)
                for t in range(NT):
                    dst = M1[:, T + E * t:T + E * (t + 1)]
                    mm(dst, beforeb[:], both[:, t, :], start=True, stop=False)
                    if t > 0:
                        mm(dst, onesb[:], both[:, 0, :], start=False, stop=False)
                    last = mm(dst, onesb[:], seen[:], start=False, stop=True)
                last.then_inc(pe_rank, 1)

            def p_kvm(s, b):
                for t in range(NT):
                    tok = slice(t * P, (t + 1) * P)
                    mm(M0[:, t * T:t * T + 192], ckvT[:, tok], wkv[:], start=True, stop=True)
                    last = mm(M0[:, t * T + 192:(t + 1) * T], xT[:, b, tok], wkr[:], start=True, stop=True)
                last.then_inc(pe_kv, 1)

            def p_q(s, b, t):
                if t == 0:
                    pe.wait_ge(dve_stat, s + 1)
                    wait(pe, logits_copied, s - 1)
                else:
                    pe.wait_ge(dve_kv, s + 1)
                mm((M1, M0)[t][:, :], cqT[:, t * P:(t + 1) * P], wq[:], start=True, stop=True).then_inc(pe_q, 1)

            def p_qT(s, b, t):
                pe.wait_ge(act_q, NT * s + t + 1)
                pe.wait_ge(q_ready, NT * s + t + 1)
                for j in range(G):
                    last = nc.tensor.transpose((M1, M0)[t][:, j * P:(j + 1) * P], qt[:, t, j].rearrange("p k d -> p (k d)"), ident[:])
                last.then_inc(pe_qT, 1)

            def p_kT(s, b):
                pe.wait_ge(k_ready, s + 1)
                pe.wait_ge(act_qT, NT * s + 1)
                for t in range(NT):
                    last = nc.tensor.transpose(M1[:, t * P:(t + 1) * P], kt[:, t].rearrange("p k d -> p (k d)"), ident[:])
                last.then_inc(pe_kT, 1)

            def scores(s, b, u):
                t, kv, j0, n = UNITS[u]
                if u == 0:
                    pe.wait_ge(act_kT, s + 1)
                    pe.wait_ge(act_qT, NT * s + NT)
                wait(pe, exped, NU * s + u - 2)
                bank = S[u % 3]
                w = P * (t + 1)
                rows = slice(kv * HD, kv * HD + HD)
                for c in range(n):
                    mm(bank[:, c * w:(c + 1) * w], qT[rows, b, t, j0 + c, :], kT[rows, b, 0:w],
                       start=(c == 0), stop=False, skip_group_check=True)
                last = mm(bank[:, :], identb[:], masks[:, t, :], start=False, stop=True, skip_group_check=True)
                last.then_inc(scored, 1)

            def turn(s, b, u):
                bank, use = t_use("p", u)
                pe.wait_ge(exped, NU * s + u + 1)
                wait(pe, t_free[bank], 4 * s + use)
                for c in range(4):
                    last = nc.tensor.transpose(TB[bank][:, c * P:(c + 1) * P], pm[:, u % 2, c * P:(c + 1) * P], ident[:])
                last.then_inc(t_full[bank], 1)

            def spread(s, b, t):
                bank, use = t_use("r", t)
                pe.wait_ge(rinv_ready, NT * s + t + 1)
                wait(pe, t_free[bank], 4 * s + use)
                for j in range(G):
                    last = nc.tensor.transpose(TB[bank][:, j * P:(j + 1) * P],
                                               rwide[:, t, j], ident[:])
                last.then_inc(t_full[bank], 1)

            def pv(s, b, t):
                for bank in range(2):
                    pe.wait_ge(t_free[bank], 4 * s + (1, 4 - bank)[t])
                if t == 0:
                    wait(pe, h_added, s)
                else:
                    pe.wait_ge(on_ready[0], s + 1)
                for kb in range(t + 1):
                    for kv in range(KVH):
                        rows = slice(kv * HD, kv * HD + HD)
                        rhs = pt0[:, kv] if t == 0 else pt1[:, kv, :, kb, :]
                        last = mm(O[rows, :], v[:, b, kb, rows], rhs, start=(kb == 0), stop=(kb == t))
                last.then_inc(pv_done[t], 1)

            def w_out_mm(s, b):
                pe.wait_ge(on_ready[1], s + 1)
                for t in range(NT):
                    dst = O[:, t * D:(t + 1) * D]
                    for j in range(G):
                        mm(dst, on[:, t, j, :], wo[:, j, :], start=(j == 0), stop=False)
                    last = mm(dst, xT[:, b, t * P:(t + 1) * P], wvo[:], start=False, stop=True)
                last.then_inc(pe_wo, 1)

            def body(s, b):
                more = not isinstance(s, int) or s + 1 < B
                s1, b1_ = s + 1, 1 - b
                routed = not isinstance(s, int) or s > 0
                scores(s, b, 0)
                scores(s, b, 1)
                scores(s, b, 2)
                if more:
                    p_a(s1, b1_)
                if routed:
                    route_turn(s - 1, 1 - b)
                turn(s, b, 0)
                turn(s, b, 1)
                scores(s, b, 3)
                if more:
                    p_b(s1, b1_)
                spread(s, b, 0)
                pv(s, b, 0)
                turn(s, b, 2)
                scores(s, b, 4)
                if more:
                    p_stats(s1, b1_)
                if routed:
                    route_logits(s - 1)
                if more:
                    p_kvm(s1, b1_)
                turn(s, b, 3)
                scores(s, b, 5)
                if more:
                    p_q(s1, b1_, 0)
                turn(s, b, 4)
                if more:
                    p_q(s1, b1_, 1)
                turn(s, b, 5)
                if more:
                    p_qT(s1, b1_, 0)
                spread(s, b, 1)
                pv(s, b, 1)
                if more:
                    p_qT(s1, b1_, 1)
                    p_kT(s1, b1_)
                w_out_mm(s, b)
                if routed:
                    route_rank(s - 1)

            p_a(0, 0)
            p_b(0, 0)
            p_stats(0, 0)
            p_kvm(0, 0)
            p_q(0, 0, 0)
            p_q(0, 0, 1)
            p_qT(0, 0, 0)
            p_qT(0, 0, 1)
            p_kT(0, 0)
            for s in (0, 1, 2):
                body(s, s % 2)
            with pe.Fori(1, 6) as i:
                body(i * 2 + 1, 1)
                body(i * 2 + 2, 0)
            for s in (13, 14, 15):
                body(s, s % 2)
            r = B - 1
            route_turn(r, 1)
            route_logits(r)
            route_rank(r)
            pe.wait_ge(c_dve, 4 * B)
            mm(M1[:, 2 * T - E:2 * T], onesb[:], seen[:], start=True, stop=True).then_inc(pe_count, 1)

            pe.wait_ge(tables_ready, 1)

            def turn_rows(j, b, turn):
                pe.wait_ge(group_in[b], 16 * (turn + 1))
                wait(pe, hT_ready, j - 1)
                for t in range(GT):
                    last = nc.tensor.transpose(XT[b % 2][:, t * P:(t + 1) * P], rows[:, b, t, 0:D], ident[:])
                last.then_inc(x_turned, 1)

            def up(j, b, turn):
                pe.wait_ge(w1_in[b], 16 * (turn + 1))
                pe.wait_ge(hT_ready, j + 1)
                for half in range(2):
                    wait(pe, hid_ready, 2 * (j - 2) + half + 1)
                    for c in range(2 * half, 2 * half + 2):
                        last = mm(HID[b % 2][half][:, (c % 2) * GR:(c % 2 + 1) * GR], w1c[:, b, c * P:(c + 1) * P],
                                  hT[:, b % 2, :], start=True, stop=True)
                    last.then_inc(hidden_done, 1)

            def down(j, b):
                e = pe.value_load(expert_i[0:1, bass.ds(j, 1)], min_val=0, max_val=E - 1)
                pe.wait_ge(hid_ready, 2 * j + 2)
                wait(pe, y_biased, j - 1)
                for t in range(GT):
                    for c in range(FC):
                        last = mm(Y[b % 2][:, t * D:(t + 1) * D], hid[:, b % 2, c, t * P:(t + 1) * P],
                                  w2s[:, bass.ds(e, 1), c, :].rearrange("p a d -> p (a d)"), start=(c == 0), stop=(c == FC - 1))
                last.then_inc(y_done, 1)

            def expert_steps(i):
                for b in range(XR):
                    j = i * XR + b
                    if not isinstance(i, int) or j + 2 < NJ:
                        turn_rows(j + 2, (b + 2) % XR, i + (b + 2) // XR)
                    if not isinstance(i, int) or j + 1 < NJ:
                        up(j + 1, (b + 1) % XR, i + (b + 1) // XR)
                    down(j, b)

            pe.wait_ge(weights_in, 32)
            turn_rows(0, 0, 0)
            turn_rows(1, 1, 0)
            up(0, 0, 0)
            expert_steps(0)
            with pe.Fori(1, NJ // XR - 1) as i:
                expert_steps(i)
            expert_steps(NJ // XR - 1)


_INS = ['x', 'L0_tok_W', 'L0_tok_b', 'L0_attn_W_DQ', 'L0_attn_W_UQ', 'L0_attn_W_QR', 'L0_attn_W_DKV', 'L0_attn_W_UK',
        'L0_attn_W_UV', 'L0_attn_W_KR', 'L0_attn_W_VR', 'L0_attn_W_O', 'L0_attn_q_ln_w', 'L0_attn_kv_ln_w',
        'L0_attn_q_head_norm_w', 'L0_attn_k_head_norm_w', 'L0_ffn_ln_g', 'L0_ffn_ln_b', 'L0_ffn_w_r', 'L0_ffn_b_r',
        'L0_ffn_W1', 'L0_ffn_b1', 'L0_ffn_W2', 'L0_ffn_b2']


def _rope_table(np):
    inv_freq = 1.0 / 500000.0 ** (np.arange(0, DR, 2, dtype=np.float32) / DR)
    freqs = np.outer(np.arange(T, dtype=np.float32), inv_freq)
    emb = np.concatenate([freqs, freqs], axis=-1)
    sign = np.concatenate([-np.ones(DR // 2, np.float32), np.ones(DR // 2, np.float32)])
    both = np.stack([np.cos(emb), np.sin(emb) * sign]).astype(np.float32)
    return np.ascontiguousarray(both.reshape(2, NT, P, DR).transpose(2, 0, 1, 3))


def kernel(**inputs):
    import numpy as _np
    import concourse.bacc as _bacc
    from concourse import mybir as _mybir
    from concourse.bass_utils import run_bass_kernel_spmd as _run

    nc = _bacc.Bacc("TRN2", target_bir_lowering=False, num_devices=1)
    arrays, args = {}, []
    host = {name: _np.ascontiguousarray(inputs[name]) for name in _INS}
    host["rope"] = _rope_table(_np)
    for name, a in host.items():
        arrays[f"in_{name}_dram"] = a
        args.append(nc.dram_tensor(f"in_{name}_dram", a.shape, _mybir.dt.from_np(a.dtype), kind="ExternalInput").ap())
    table = nc.dram_tensor("row_table", (VOCAB, D), _mybir.dt.float32, kind="Internal").ap()
    xs = nc.dram_tensor("expert_rows", (E * REGION, ROW), _mybir.dt.float32, kind="Internal").ap()
    ys = nc.dram_tensor("expert_outputs", (K * N, D), _mybir.dt.float32, kind="Internal").ap()
    out = nc.dram_tensor("out_0_dram", (B, T, D), _mybir.dt.float32, kind="ExternalOutput").ap()
    tower_kernel(nc, *args, table, xs, ys, out)
    r = _run(nc, [arrays], core_ids=[0])
    return r.results[0]["out_0_dram"]
```

```python
import concourse.bass as bass
from concourse import mybir
from contextlib import ExitStack

F32 = mybir.dt.float32
BF16 = mybir.dt.bfloat16
I32 = mybir.dt.int32
U32 = mybir.dt.uint32
ALU = mybir.AluOpType
ACT = mybir.ActivationFunctionType
AX = mybir.AxisListType

P = 128
D = 128
B, T = 16, 256
NT = T // P
TILES = B * NT
VOCAB = 50257
H, KVH, HD, DN, DR = 8, 2, 64, 32, 32
G = H // KVH
RQ, RKV = 64, 128

CW = 1024
CJ = CW // P
CHUNKS = VOCAB // CW
TAIL = VOCAB - CHUNKS * CW
RING = 8
ROUNDS = CHUNKS // RING
assert CHUNKS == ROUNDS * RING + 1 and TAIL <= P

E, K, FF = 8, 2, 512
FC = FF // P
N = B * T
GT = 2
GR = GT * P
REGION = N + GR
NJ = N * K // GR + E - 1
OC = 8
XR = 4
ROW = D + 4
GATE, DEST = D, D + 1
TURNS = NJ // XR
LEFT = NJ % XR
assert NJ * GR >= N * K + E * (GR - 1) - (GR - 1) and GR & (GR - 1) == 0

UNITS = [(0, 0, 0, 4), (0, 1, 0, 4), (1, 0, 0, 2), (1, 0, 2, 2), (1, 1, 0, 2), (1, 1, 2, 2)]
NU = len(UNITS)


def wait(eng, sem, value):
    if isinstance(value, int) and value <= 0:
        return
    eng.wait_ge(sem, value)


def stand_alone(eng, sem):
    eng.sem_inc(sem, 1)


def tower_kernel(nc, x, tok_W, tok_b, W_DQ, W_UQ, W_QR, W_DKV, W_UK, W_UV, W_KR, W_VR, W_O, q_ln_w,
                 kv_ln_w, qh_w, kh_w, ln_g, ln_b, w_r, b_r, W1, b1, W2, b2, rope, table,
                 xs, ys, out):
    with ExitStack() as ctx:
        def sb(name, shape, dt=F32):
            return ctx.enter_context(nc.sbuf_tensor(name, shape, dt))

        def sem(name):
            return ctx.enter_context(nc.semaphore(name))

        w_in = sb("w_in", [P, RING, CW])
        w_out = sb("w_out", [P, RING, CJ, D])
        ident = sb("ident", [P, P])
        identb = sb("identb", [P, P], BF16)
        masks = sb("masks", [P, 4 * P], BF16)
        maskf = sb("maskf", [P, P])
        ids = sb("ids", [P, TILES], I32)
        ids_now = sb("ids_now", [P, 2, NT], I32)
        tokb = sb("tokb", [P, D])
        cossin = sb("cossin", [P, 2, NT, DR])
        wdq = sb("wdq", [P, RQ])
        wdkv = sb("wdkv", [P, RKV])
        wkr = sb("wkr", [P, KVH * DR])
        wq_raw = sb("wq_raw", [RQ, G, KVH, HD])
        wq = sb("wq", [RQ, G * KVH * HD])
        wkv_raw = sb("wkv_raw", [P, KVH * DN + KVH * HD])
        wkv = sb("wkv", [P, KVH * DN + KVH * HD])
        wvr = sb("wvr", [P, G, KVH, HD])
        wvrT = sb("wvrT", [P, G, D])
        wo = sb("wo", [P, G, D])
        wvo = sb("wvo", [P, D])
        qln = sb("qln", [RQ, 1])
        kvln = sb("kvln", [P, 1])
        hw2 = sb("hw2", [P, 2])
        khw = sb("khw", [P, 1])
        mean_w = sb("mean_w", [P, 2])
        neg_half = sb("neg_half", [P, 16])
        gat = sb("gat", [P, 2, NT, D])
        f = sb("f", [P, NT, D])
        bst = sb("bst", [P, NT, 6])
        mv = sb("mv", [P, NT, 2])
        est = sb("est", [P, 10, NT])
        hall = sb("hall", [P, TILES, D])
        xn = sb("xn", [P, 2, NT, D])
        xT = sb("xT", [P, 2, T])
        sqc = sb("sqc", [P, 2, T])
        cqT = sb("cqT", [RQ, T])
        ckvT = sb("ckvT", [P, T])
        em = sb("em", [P, NT, 2])
        skv = sb("skv", [P, NT])
        epsq = sb("epsq", [P, NT])
        qt = sb("qt", [P, NT, G, KVH, HD])
        kt = sb("kt", [P, NT, KVH, HD])
        v = sb("v", [P, 2, NT, KVH * HD])
        rope_a = sb("rope_a", [P, NT, H, DR])
        rope_b = sb("rope_b", [P, NT, H, DR])
        krope_a = sb("krope_a", [P, NT, KVH, DR])
        krope_b = sb("krope_b", [P, NT, KVH, DR])
        qsq = sb("qsq", [P, NT, H, HD])
        qss = sb("qss", [P, NT, H])
        rqv = sb("rqv", [P, NT, H])
        rq = sb("rq", [P, 2, NT, G, KVH])
        ksq = sb("ksq", [P, NT, KVH, HD])
        kss = sb("kss", [P, NT * KVH])
        rkv = sb("rkv", [P, NT * KVH])
        rk = sb("rk", [P, NT * KVH])
        qT = sb("qT", [P, 2, NT, G, P])
        kT = sb("kT", [P, 2, T])
        negmax = sb("negmax", [P, NU, G])
        nbias = sb("nbias", [P, NU, G])
        pm = sb("pm", [P, 2, 512])
        rsum = sb("rsum", [P, NT, G, KVH])
        rinv = sb("rinv", [P, NT, G, KVH])
        rwide = sb("rwide", [P, NT, G, KVH * HD])
        rb = sb("rb", [P, NT, 512])
        pt0 = sb("pt0", [P, KVH, G, P])
        pt1 = sb("pt1", [P, KVH, G, NT, P])
        on = sb("on", [P, NT, G, P])

        iota8 = sb("iota8", [P, E])
        region8 = sb("region8", [P, E])
        before = sb("before", [P, P])
        beforeb = sb("beforeb", [P, P], BF16)
        onesb = sb("onesb", [P, P], BF16)
        lng = sb("lng", [P, 1])
        lnb = sb("lnb", [P, 1])
        wrT = sb("wrT", [P, E])
        br = sb("br", [P, E])
        bst2 = sb("bst2", [P, NT, 6])
        mv2 = sb("mv2", [P, NT, 2])
        rst = sb("rst", [P, 9, NT])
        row = sb("row", [P, 2, NT, K, ROW])
        dest = sb("dest", [P, NT, K])
        hfT = sb("hfT", [P, T])
        lg = sb("lg", [P, NT, E])
        mx8 = sb("mx8", [P, NT, 8])
        ix8 = sb("ix8", [P, NT, 8], U32)
        ixf = sb("ixf", [P, NT, K])
        chosen = sb("chosen", [P, NT, K, E])
        both = sb("both", [P, NT, E], BF16)
        seen = sb("seen", [P, E], BF16)
        dlog = sb("dlog", [P, NT])
        eg = sb("eg", [P, NT])
        eg1 = sb("eg1", [P, NT])
        pos = sb("pos", [P, NT, E])
        posk = sb("posk", [P, NT, K, E])
        slotf = sb("slotf", [P, NT * K])
        slot = sb("slot", [P, 2, NT * K], I32)
        cnt = sb("cnt", [1, E])
        cnti = sb("cnti", [1, E], I32)
        cntt = sb("cntt", [1, E], I32)
        ntile = sb("ntile", [1, E])
        tend = sb("tend", [1, E])
        tbase = sb("tbase", [1, E])
        zero8 = sb("zero8", [1, E])
        gelu_of_zero = sb("gelu_of_zero", [1, E])
        iotaj = sb("iotaj", [1, NJ])
        je = sb("je", [1, NJ, E])
        jexp = sb("jexp", [1, NJ])
        jvalid = sb("jvalid", [1, NJ])
        jstart = sb("jstart", [1, NJ])
        start_i = sb("start_i", [1, NJ], I32)
        expert_i = sb("expert_i", [1, NJ], I32)
        padrow = sb("padrow", [1, E])
        pad_i = sb("pad_i", [1, E], I32)
        padding = sb("padding", [P, GT, ROW])
        w_flat = w_out[:, :, :, :].rearrange("p u j d -> p (u j d)")
        w2s = w_flat[:, 0:E * FC * D].rearrange("p (e c d) -> p e c d", e=E, c=FC)
        w1c = w_flat[:, E * FC * D:E * FC * D + XR * FF].rearrange("p (r f) -> p r f", r=XR)
        x_flat = w_in[:, :, :].rearrange("p u c -> p (u c)")
        at = [0]

        def carve(n):
            at[0] += n
            return x_flat[:, at[0] - n:at[0]]

        rows = carve(XR * GT * ROW).rearrange("p (r t c) -> p r t c", r=XR, t=GT)
        hT = carve(2 * GR).rearrange("p (r n) -> p r n", r=2)
        hid = carve(2 * FC * GR).rearrange("p (r c n) -> p r c n", r=2, c=FC)
        yt = carve(2 * GT * D).rearrange("p (r t d) -> p r t d", r=2, t=GT)
        yb = carve(XR * GT * D).rearrange("p (r t d) -> p r t d", r=XR, t=GT)
        b2c = carve(XR * D).rearrange("p (r d) -> p r d", r=XR)
        b1s = sb("b1s", [P, E, FC])
        b2s = sb("b2s", [P, E, D])
        b1c = sb("b1c", [P, XR, FC])
        where = sb("where", [P, XR, GT], I32)

        banks = [ctx.enter_context(nc.psum_tensor(f"bank{i}", [P, 512], F32)) for i in range(8)]
        S = banks[0:3]
        TB = banks[3:5]
        O, M0, M1 = banks[5:8]
        HID, XT, Y = (banks[0:2], banks[2:4]), banks[4:6], banks[6:8]

        QT = TILES // OC
        y_parts = w_in[:, :, :].rearrange("p u c -> p (u c)").rearrange("p (k c t d) -> p k c t d", k=K, c=OC, t=QT)

        chunk_in = [sem(f"chunk_in{u}") for u in range(RING)]
        chunk_out = [sem(f"chunk_out{u}") for u in range(RING)]
        turned = sem("turned")
        even_copied = sem("even_copied")
        odd_copied = sem("odd_copied")
        consts_in = sem("consts_in")
        ids_in = sem("ids_in")
        pool_init = sem("pool_init")
        dve_init = sem("dve_init")
        setup_pe = sem("setup_pe")
        setup_act = sem("setup_act")
        rows_in = [sem("rows_in0"), sem("rows_in1")]
        ids_copied = sem("ids_copied")
        e_pool = sem("e_pool")
        e_dve = sem("e_dve")
        embedded = sem("embedded")
        x_ready = sem("x_ready")
        f_ready = sem("f_ready")
        mv_ready = sem("mv_ready")
        pe_xT = sem("pe_xT")
        act_xT = sem("act_xT")
        pe_c = sem("pe_c")
        act_sq = sem("act_sq")
        pe_stat = sem("pe_stat")
        pe_kv = sem("pe_kv")
        dve_stat = sem("dve_stat")
        skv_ready = sem("skv_ready")
        dve_kv = sem("dve_kv")
        p_pool = sem("p_pool")
        pe_q = sem("pe_q")
        act_q = sem("act_q")
        dve_rope = sem("dve_rope")
        q_ready = [sem("q_ready0"), sem("q_ready1")]
        kt_ready = sem("kt_ready")
        ksq_ready = sem("ksq_ready")
        kss_ready = sem("kss_ready")
        qss_ready = sem("qss_ready")
        rq_ready = sem("rq_ready")
        k_ready = sem("k_ready")
        pe_qT = sem("pe_qT")
        act_qT = sem("act_qT")
        pe_kT = sem("pe_kT")
        act_kT = sem("act_kT")
        scored = sem("scored")
        max_done = sem("max_done")
        bias_ready = sem("bias_ready")
        exped = sem("exped")
        t_full = [sem("t_full0"), sem("t_full1")]
        t_free = [sem("t_free0"), sem("t_free1")]
        rinv_done = sem("rinv_done")
        rinv_ready = sem("rinv_ready")
        pv_done = [sem("pv_done0"), sem("pv_done1")]
        on_ready = [sem("on_ready0"), sem("on_ready1")]
        pe_wo = sem("pe_wo")
        h_added = sem("h_added")
        stored = sem("stored")
        weights_in = sem("weights_in")
        r_stats = sem("r_stats")
        mv2_ready = sem("mv2_ready")
        r_pool = sem("r_pool")
        coef_ready = sem("coef_ready")
        hh_ready = sem("hh_ready")
        base_ready = sem("base_ready")
        pe_h = sem("pe_h")
        act_h = sem("act_h")
        pe_logits = sem("pe_logits")
        logits_copied = sem("logits_copied")
        r_dve = sem("r_dve")
        g_dve = sem("g_dve")
        dlog_ready = sem("dlog_ready")
        eg_ready = sem("eg_ready")
        both_ready = sem("both_ready")
        pe_rank = sem("pe_rank")
        rank_copied = sem("rank_copied")
        slot_ready = sem("slot_ready")
        scattered = [sem("scattered0"), sem("scattered1")]
        row_full = sem("row_full")
        pe_count = sem("pe_count")
        c_dve = sem("c_dve")
        t_dve = sem("t_dve")
        pads_known = sem("pads_known")
        tables_ready = sem("tables_ready")
        padded = sem("padded")
        group_in = [sem(f"group_in{b}") for b in range(XR)]
        w1_in = [sem(f"w1_in{b}") for b in range(XR)]
        biases_ready = sem("biases_ready")
        x_turned = sem("x_turned")
        hT_ready = sem("hT_ready")
        hidden_done = sem("hidden_done")
        hid_ready = sem("hid_ready")
        y_done = sem("y_done")
        y_biased = sem("y_biased")
        y_ready = sem("y_ready")
        y_out = [sem(f"y_out{b}") for b in range(XR)]
        y_in = [sem(f"y_in{c}") for c in range(OC)]
        y_add = sem("y_add")
        y_sum = sem("y_sum")
        passed = sem("passed")

        block = ctx.enter_context(nc.Block())

        SMALL = 26

        def chunk_rows(n):
            return table[bass.ds(n * CW, CW), :].rearrange("(p j) d -> p (j d)", j=CJ)

        T_USES = [("p", 0), ("p", 1), ("r", 0), ("p", 2), ("p", 3), ("p", 4), ("p", 5), ("r", 1)]

        def t_use(kind, n):
            k = T_USES.index((kind, n))
            return k % 2, k // 2

        def pt_evacuate(eng, copy, s, u):
            t, kv, j0, n = UNITS[u]
            bank, use = t_use("p", u)
            eng.wait_ge(t_full[bank], 4 * s + use + 1)
            wait(eng, pv_done[t], s)
            if t == 0:
                dst = pt0[:, kv].rearrange("p j q -> p (j q)")
            else:
                dst = pt1[:, kv, j0:j0 + n].rearrange("p j k q -> p (j k q)")
            copy(dst, TB[bank][:, :]).then_inc(t_free[bank], 1)

        def pad_experts(eng, experts):
            eng.wait_ge(pads_known, 1)
            for e in experts:
                at = eng.value_load(pad_i[0:1, e:e + 1], min_val=0, max_val=E * REGION - GR)
                eng.dma_start(xs[bass.ds(at, GR), :].rearrange("(p t) c -> p t c", t=GT), padding[:]).then_inc(padded, 16)

        @block.sync
        def _(sp):
            def load(n, u):
                sp.dma_start(w_in[:, u, :], tok_W[:, bass.ds(n * CW, CW)]).then_inc(chunk_in[u], 16)

            def store(n, u):
                sp.wait_ge(even_copied, n + 1)
                sp.wait_ge(odd_copied, n + 1)
                sp.dma_start(chunk_rows(n), w_out[:, u].rearrange("p j d -> p (j d)")).then_inc(chunk_out[u], 16)

            for u in range(RING):
                load(u, u)
            with sp.Fori(0, ROUNDS - 1) as i:
                for u in range(RING):
                    store(i * RING + u, u)
                    load(i * RING + u + RING, u)
            for u in range(RING):
                n = (ROUNDS - 1) * RING + u
                store(n, u)
                if u == 0:
                    load(n + RING, u)
                if u == 1:
                    sp.dma_start(w_in[:, u, 0:TAIL], tok_W[:, CHUNKS * CW:VOCAB]).then_inc(chunk_in[u], 16)
            store(CHUNKS - 1, 0)
            sp.wait_ge(even_copied, CHUNKS + 1)
            sp.dma_start(table[CHUNKS * CW:VOCAB, :], w_out[0:TAIL, 1, 0, :]).then_inc(chunk_out[1], 16)

            for u in range(RING):
                sp.wait_ge(chunk_out[u], 16 * (ROUNDS + (u < 2)))
            for b in range(2):
                sp.wait_ge(rows_in[b], 16 * NT)
            sp.dma_start(w2s[:], W2.rearrange("e (c p) d -> p e c d", p=P)).then_inc(weights_in, 16)
            sp.dma_start(b2s[:], b2.rearrange("(a e) d -> a e d", a=1).to_broadcast([P, E, D])).then_inc(weights_in, 16)

            pad_experts(sp, range(0, E // 2))

            def load_w1(j, b):
                e = sp.value_load(expert_i[0:1, bass.ds(j, 1)], min_val=0, max_val=E - 1)
                wait(sp, hidden_done, 2 * (j - XR + 1))
                sp.dma_start(w1c[:, b, :], W1[bass.ds(e, 1)].rearrange("a d f -> d (a f)")).then_inc(w1_in[b], 16)

            def load_rows(j, b):
                start = sp.value_load(start_i[0:1, bass.ds(j, 1)], min_val=0, max_val=E * REGION - GR)
                if isinstance(j, int) and j == 0:
                    sp.wait_ge(padded, 16 * E)
                    for c in range(2):
                        sp.wait_ge(scattered[c], 16 * NT * K * (B // 2))
                wait(sp, y_ready, j - XR + 1)
                sp.dma_start(rows[:, b], xs[bass.ds(start, GR), :].rearrange("(p t) c -> p t c", t=GT)).then_inc(group_in[b], 16)

            sp.wait_ge(tables_ready, 1)
            load_w1(0, 0)
            load_w1(1, 1)
            for b in range(XR):
                load_rows(b, b)
            for b in range(2, XR):
                load_w1(b, b)
            with sp.Fori(1, TURNS) as i:
                for b in range(XR):
                    load_rows(i * XR + b, b)
                    load_w1(i * XR + b, b)
            for b in range(LEFT):
                load_rows(TURNS * XR + b, b)
                load_w1(TURNS * XR + b, b)

            for b in range(XR):
                sp.wait_ge(y_out[b], 16 * GT * (TURNS + (b < LEFT)))
            for c in range(OC):
                for k in range(K):
                    r0 = k * N + c * QT * P
                    sp.dma_start(y_parts[:, k, c], ys[r0:r0 + QT * P, :].rearrange("(t p) d -> p t d", p=P)).then_inc(y_in[c], 16)
            flat = out.rearrange("b (t p) d -> p (b t) d", p=P)
            for c in range(OC):
                sp.wait_ge(y_sum, c + 1)
                sp.dma_start(flat[:, c * QT:(c + 1) * QT, :], hall[:, c * QT:(c + 1) * QT, :]).then_inc(stored, 16)
            sp.wait_ge(stored, 16 * OC)

        @block.gpsimd
        def _(pool):
            nc.gpsimd.memset(ident[:], 0.0).then_inc(pool_init, 1)
            nc.gpsimd.memset(maskf[:], 0.0).then_inc(pool_init, 1)
            nc.gpsimd.memset(mean_w[:, 0:1], 1.0 / RQ)
            nc.gpsimd.memset(mean_w[:, 1:2], 1.0 / RKV)
            nc.gpsimd.memset(before[:], 1.0)
            nc.gpsimd.memset(onesb[:], 1.0)
            nc.gpsimd.memset(seen[:], 0.0)
            nc.gpsimd.memset(zero8[:], 0.0)
            nc.gpsimd.memset(padding[:], 0.0)
            nc.gpsimd.memset(row[:], 0.0)
            nc.gpsimd.iota(iota8[:], [[1, E]], base=0, channel_multiplier=0, allow_small_or_imprecise_dtypes=True)
            nc.gpsimd.iota(region8[:], [[REGION // P, E]], base=0, channel_multiplier=0, allow_small_or_imprecise_dtypes=True)
            nc.gpsimd.iota(iotaj[:], [[1, NJ]], base=0, channel_multiplier=0, allow_small_or_imprecise_dtypes=True)
            nc.gpsimd.iota(dest[:], [[P, NT], [N, K]], base=0, channel_multiplier=1, allow_small_or_imprecise_dtypes=True)
            nc.gpsimd.memset(neg_half[:], -0.5).then_inc(pool_init, 1)
            pool.wait_ge(pool_init, 3)
            nc.gpsimd.affine_select(out=ident[:], in_=ident[:], compare_op=ALU.not_equal, fill=1.0, base=0,
                                    pattern=[[-1, P]], channel_multiplier=1)
            nc.gpsimd.affine_select(out=before[:], in_=before[:], compare_op=ALU.is_ge, fill=0.0, base=-1,
                                    pattern=[[1, P]], channel_multiplier=-1)
            nc.gpsimd.iota(padding[:, :, DEST], [[P, GT]], base=K * N, channel_multiplier=1, allow_small_or_imprecise_dtypes=True)
            nc.gpsimd.affine_select(out=maskf[:], in_=maskf[:], compare_op=ALU.is_ge, fill=-1e30, base=0,
                                    pattern=[[-1, P]], channel_multiplier=1).then_inc(pool_init, 1)
            pool.wait_ge(ids_in, 16)
            for u in range(RING):
                pool.wait_ge(chunk_out[u], 16 * (ROUNDS + (u < 2)))

            two_halves = neg_half[:, 0:2 * NT].rearrange("p (a t) -> p a t", t=NT)

            def gather(s, b):
                nc.gpsimd.tensor_copy(ids_now[:, b, :], ids[:, bass.ds(s * NT, NT)]).then_inc(ids_copied, 1)
                pool.wait_ge(ids_copied, s + 1)
                stand_alone(pool, passed)
                for t in range(NT):
                    nc.gpsimd.indirect_dma_start(
                        out=gat[:, b, t, :], out_offset=None, in_=table[:, :],
                        in_offset=bass.IndirectOffsetOnAxis(ap=ids_now[:, b, t:t + 1], axis=0)).then_inc(rows_in[b], 16)

            E_STEPS = 10

            def embed_f(s, b, half):
                pool.wait_ge(rows_in[b], 16 * NT * (half + 1))
                wait(pool, x_ready, s)
                nc.gpsimd.tensor_tensor(out=f[:], in0=gat[:, b], in1=tokb[:].unsqueeze(1).to_broadcast([P, NT, D]),
                                        op=ALU.add).then_inc(f_ready, 1)

            def embed_x(s, b):
                k = [0]

                def link(ins):
                    k[0] += 1
                    ins.then_inc(e_pool, 1)
                    pool.wait_ge(e_pool, E_STEPS * s + k[0])
                    if k[0] in (2, 6, E_STEPS):
                        stand_alone(pool, passed)

                def tt(o, a, c, op):
                    link(nc.gpsimd.tensor_tensor(out=o, in0=a, in1=c, op=op))

                mean, var = mv[:, :, 0], mv[:, :, 1]
                e = [est[:, i, :] for i in range(10)]
                pool.wait_ge(mv_ready, s + 1)
                wait(pool, x_ready, s)
                tt(e[0], mean, mean, ALU.mult)
                tt(e[0], e[0], var, ALU.add)
                link(nc.gpsimd.tensor_scalar(out=e[1], in0=e[0], scalar1=float(D), scalar2=1e-24, op0=ALU.mult, op1=ALU.max))
                tt(e[2], e[1], neg_half[:, 0:NT], ALU.pow)
                tt(e[3], e[2], e[2], ALU.mult)
                tt(e[3], e[3], var, ALU.mult)
                link(nc.gpsimd.tensor_scalar(out=e[4], in0=e[3], scalar1=1e-5, scalar2=None, op0=ALU.add))
                tt(e[5], e[4], neg_half[:, 0:NT], ALU.pow)
                tt(e[6], e[2], e[5], ALU.mult)
                tt(e[7], mean, e[6], ALU.mult)
                assert k[0] == E_STEPS
                nc.gpsimd.tensor_tensor(out=hall[:, bass.ds(s * NT, NT), :], in0=f[:],
                                        in1=e[2].unsqueeze(2).to_broadcast([P, NT, D]), op=ALU.mult).then_inc(embedded, 1)

            P_STEPS = 4

            def latent_norms(s):
                pool.wait_ge(dve_stat, s + 1)
                nc.gpsimd.tensor_tensor(out=skv[:], in0=em[:, :, 1], in1=neg_half[:, 0:NT], op=ALU.pow).then_inc(skv_ready, 1)
                nc.gpsimd.tensor_scalar(out=epsq[:], in0=em[:, :, 0], scalar1=1e-6 * HD, scalar2=None, op0=ALU.mult).then_inc(p_pool, 1)

            def project(s, b):
                k = [1]

                def link(ins):
                    k[0] += 1
                    ins.then_inc(p_pool, 1)
                    pool.wait_ge(p_pool, P_STEPS * s + k[0])

                pool.wait_ge(dve_kv, s + 1)
                nc.gpsimd.tensor_tensor(out=kt[:, :, :, DN:HD], in0=krope_a[:], in1=krope_b[:], op=ALU.add).then_inc(kt_ready, 1)
                pool.wait_ge(dve_rope, NT * s + 1)
                nc.gpsimd.tensor_tensor(out=qt[:, 0].rearrange("p g k d -> p (g k) d")[:, :, DN:HD], in0=rope_a[:, 0],
                                        in1=rope_b[:, 0], op=ALU.add).then_inc(q_ready[0], 1)
                pool.wait_ge(kss_ready, s + 1)
                stand_alone(pool, passed)
                link(nc.gpsimd.tensor_scalar(out=rkv[:], in0=kss[:], scalar1=1.0 / HD, scalar2=1e-6, op0=ALU.mult, op1=ALU.add))
                link(nc.gpsimd.tensor_tensor(out=rk[:], in0=rkv[:], in1=neg_half[:, 0:NT * KVH], op=ALU.pow))
                kflat = kt[:].rearrange("p t k d -> p (t k) d")
                nc.gpsimd.tensor_tensor(out=kflat, in0=kflat, in1=rk[:].unsqueeze(2).to_broadcast([P, NT * KVH, HD]),
                                        op=ALU.mult).then_inc(k_ready, 1)
                pool.wait_ge(qss_ready, s + 1)
                link(nc.gpsimd.tensor_tensor(out=rqv[:], in0=qss[:], in1=epsq[:].unsqueeze(2).to_broadcast([P, NT, H]), op=ALU.add))
                assert k[0] == P_STEPS
                nc.gpsimd.tensor_tensor(out=rq[:, b].rearrange("p t g k -> p (t g k)"), in0=rqv[:].rearrange("p t h -> p (t h)"),
                                        in1=neg_half[:, 0:NT * H], op=ALU.pow).then_inc(rq_ready, 1)

            R_STEPS = 3

            def route_coefficients(r):
                k = [0]

                def link(ins):
                    k[0] += 1
                    ins.then_inc(r_pool, 1)
                    pool.wait_ge(r_pool, R_STEPS * r + k[0])

                def tt(o, a, c, op):
                    return nc.gpsimd.tensor_tensor(out=o, in0=a, in1=c, op=op)

                pool.wait_ge(mv2_ready, r + 1)
                wait(pool, base_ready, r)
                mean = mv2[:, :, 0]
                e = [rst[:, i, :] for i in range(9)]
                link(tt(rst[:, 2:4, :], rst[:, 0:2, :], two_halves, ALU.pow))
                link(tt(e[5], e[2], e[3], ALU.mult))
                tt(e[6], mean, e[5], ALU.mult)
                link(tt(e[7], mean, e[2], ALU.mult))
                stand_alone(pool, passed)
                nc.gpsimd.tensor_scalar(out=e[7], in0=e[7], scalar1=-1.0, scalar2=None, op0=ALU.mult)
                assert k[0] == R_STEPS
                nc.gpsimd.tensor_scalar(out=e[8], in0=e[2], scalar1=1.0, scalar2=None, op0=ALU.add).then_inc(coef_ready, 1)

            def complete_rows(r, b):
                pool.wait_ge(hh_ready, r + 1)
                stand_alone(pool, passed)
                nc.gpsimd.tensor_copy(row[:, b, :, :, DEST], dest[:]).then_inc(row_full, 1)
                pool.wait_ge(row_full, 2 * r + 1)
                stand_alone(pool, passed)
                nc.gpsimd.tensor_scalar(out=dest[:], in0=dest[:], scalar1=float(T), scalar2=None, op0=ALU.add).then_inc(row_full, 1)
                pool.wait_ge(row_full, 2 * r + 2)
                pool.wait_ge(slot_ready, r + 1)
                stand_alone(pool, passed)

            def dispatch(b, t):
                for k in range(K):
                    i = t * K + k
                    nc.gpsimd.indirect_dma_start(
                        out=xs[:, :], out_offset=bass.IndirectOffsetOnAxis(ap=slot[:, b, i:i + 1], axis=0),
                        in_=row[:, b, t, k, :], in_offset=None).then_inc(scattered[b], 16)

            def body(s, b, half):
                if not isinstance(s, int) or s + 3 < B:
                    gather(s + 3, 1 - b)
                if not isinstance(s, int) or s + 2 < B:
                    embed_f(s + 2, b, half + 1)
                if not isinstance(s, int) or s > 0:
                    route_coefficients(s - 1)
                if not isinstance(s, int) or s > 1:
                    complete_rows(s - 2, b)
                    dispatch(b, 0)
                if not isinstance(s, int) or s + 1 < B:
                    latent_norms(s + 1)
                if not isinstance(s, int) or s > 1:
                    dispatch(b, 1)
                if not isinstance(s, int) or s + 1 < B:
                    project(s + 1, 1 - b)
                if not isinstance(s, int) or s + 2 < B:
                    embed_x(s + 2, b)

            gather(0, 0)
            gather(1, 1)
            pool.wait_ge(consts_in, 16 * SMALL)
            embed_f(0, 0, 0)
            embed_x(0, 0)
            gather(2, 0)
            latent_norms(0)
            embed_f(1, 1, 0)
            project(0, 0)
            embed_x(1, 1)
            for s in (0, 1, 2):
                body(s, s % 2, s // 2)
            with pool.Fori(1, 6) as i:
                body(i * 2 + 1, 1, i)
                body(i * 2 + 2, 0, i + 1)
            for s in (13, 14, 15):
                body(s, s % 2, s // 2)
            route_coefficients(B - 1)
            for r, b in ((B - 2, 0), (B - 1, 1)):
                complete_rows(r, b)
                dispatch(b, 0)
                dispatch(b, 1)

            def scatter_y(j, b):
                pool.wait_ge(y_ready, j + 1)
                stand_alone(pool, passed)
                for t in range(GT):
                    nc.gpsimd.indirect_dma_start(
                        out=ys[:, :], out_offset=bass.IndirectOffsetOnAxis(ap=where[:, b, t:t + 1], axis=0), in_=yb[:, b, t, :],
                        in_offset=None, bounds_check=K * N - 1, oob_is_err=False).then_inc(y_out[b], 16)

            with pool.Fori(0, TURNS) as i:
                for b in range(XR):
                    scatter_y(i * XR + b, b)
            for b in range(LEFT):
                scatter_y(TURNS * XR + b, b)

        @block.scalar
        def _(act):
            def small(dst, src):
                act.dma_start(dst, src).then_inc(consts_in, 16)

            def row_(a):
                return a.rearrange("(a n) -> a n", a=1)

            def col(a):
                return a.rearrange("(n a) -> n a", a=1)

            with nc.allow_non_contiguous_dma(reason="small tables"):
                act.dma_start(ids[:, :].rearrange("p (b t) -> p b t", b=B), x.rearrange("b (t p) -> p b t", p=P)).then_inc(ids_in, 16)
                small(tokb[:], row_(tok_b).to_broadcast([P, D]))
                small(cossin[:], rope)
                small(wdq[:], W_DQ)
                small(wdkv[:], W_DKV)
                small(wkr[:], W_KR)
                for a in range(KVH):
                    small(wq_raw[:, :, a, 0:DN], W_UQ.rearrange("c (a j d) -> c a j d", a=KVH, j=G)[:, a])
                    small(wq_raw[:, :, a, DN:HD], W_QR.rearrange("c (a j d) -> c a j d", a=KVH, j=G)[:, a])
                    small(wvr[:, :, a, :], W_VR.rearrange("c (a j d) -> c a j d", a=KVH, j=G)[:, a])
                    small(wo[HD * a:HD * a + HD, :, :], W_O.rearrange("(a j d) n -> a d j n", a=KVH, j=G)[a])
                small(wkv_raw[:, 0:KVH * DN], W_UK)
                small(wkv_raw[:, KVH * DN:], W_UV)
                small(qln[:], col(q_ln_w))
                small(kvln[:], col(kv_ln_w))
                small(lng[:], col(ln_g))
                small(lnb[:], col(ln_b))
                small(br[:], row_(b_r).to_broadcast([P, E]))
                small(wrT[:], w_r.rearrange("e d -> d e"))
                small(b1s[:].rearrange("p e c -> p (e c)"), b1.rearrange("e (c p) -> p (e c)", p=P))
                for a in range(KVH):
                    small(hw2[HD * a:HD * a + HD, 0:1], col(qh_w))
                    small(hw2[HD * a:HD * a + HD, 1:2], col(kh_w))

            def copy(dst, src):
                return nc.scalar.activation(dst, src, ACT.Copy)

            def table_chunk(n, u, i):
                act.wait_ge(turned, 2 * n + 1)
                wait(act, chunk_out[u], 16 * i)
                copy(w_out[:, u, 0:4, :].rearrange("p j d -> p (j d)"), banks[2 * (u % 4)][:, :]).then_inc(even_copied, 1)

            for u in range(RING):
                table_chunk(u, u, 0)
            with act.Fori(1, ROUNDS) as i:
                for u in range(RING):
                    table_chunk(i * RING + u, u, i)
            table_chunk(CHUNKS - 1, 0, ROUNDS)
            act.wait_ge(turned, 2 * CHUNKS + 1)
            wait(act, chunk_out[1], 16 * ROUNDS)
            copy(w_out[0:TAIL, 1, 0, :], banks[2][0:TAIL, 0:D]).then_inc(even_copied, 1)

            act.wait_ge(setup_pe, 1)
            copy(wvrT[:].rearrange("p j d -> p (j d)"), banks[0][:, :]).then_inc(setup_act, 1)
            act.wait_ge(setup_pe, 2)
            copy(wvo[:], banks[1][:, 0:D]).then_inc(setup_act, 1)

            def p_xT(s, b):
                act.wait_ge(pe_xT, s + 1)
                wait(act, pe_wo, NT * (s - 1))
                copy(xT[:, b, :], M0[:, 0:T]).then_inc(act_xT, 1)

            def p_sq(s, b):
                act.wait_ge(pe_c, s + 1)
                nc.scalar.activation(sqc[0:RQ, 0, :], M1[0:RQ, 0:T], ACT.Square)
                nc.scalar.activation(sqc[:, 1, :], M1[:, T:2 * T], ACT.Square)
                copy(cqT[:], M1[0:RQ, 0:T])
                copy(ckvT[:], M1[:, T:2 * T]).then_inc(act_sq, 1)

            def p_q(s, b, t):
                M = (M1, M0)[t]
                act.wait_ge(pe_q, NT * s + t + 1)
                wait(act, qss_ready, s)
                nc.scalar.activation(qsq[:, t].rearrange("p h d -> p (h d)"), M[:, :], ACT.Square)
                copy(qt[:, t].rearrange("p g k d -> p (g k) d")[:, :, 0:DN],
                     M[:, :].rearrange("p (h d) -> p h d", d=HD)[:, :, 0:DN]).then_inc(act_q, 1)

            def p_ksq(s):
                act.wait_ge(kt_ready, s + 1)
                wait(act, kss_ready, s)
                nc.scalar.activation(ksq[:], kt[:], ACT.Square).then_inc(ksq_ready, 1)

            def p_qT(s, b, t):
                act.wait_ge(pe_qT, NT * s + t + 1)
                copy(qT[:, b, t].rearrange("p j q -> p (j q)"), (M1, M0)[t][:, :]).then_inc(act_qT, 1)

            def p_kT(s, b):
                act.wait_ge(pe_kT, s + 1)
                nc.scalar.activation(kT[:, b, :], M1[:, 0:T], ACT.Copy, scale=khw[:, 0:1]).then_inc(act_kT, 1)

            def exps(s, b, u):
                t, kv, j0, n = UNITS[u]
                act.wait_ge(bias_ready, NU * s + u + 1)
                before = (u - 2) % NU
                bank, use = t_use("p", before)
                wait(act, t_full[bank], 4 * (s - (u < 2)) + use + 1)
                w = P * (t + 1)
                for c in range(n):
                    last = nc.scalar.activation(pm[:, u % 2, c * w:(c + 1) * w], S[u % 3][:, c * w:(c + 1) * w], ACT.Exp,
                                                bias=nbias[:, u, c:c + 1], scale=rq[:, b, t, j0 + c, kv:kv + 1],
                                                accum_out=rsum[:, t, j0 + c, kv:kv + 1])
                last.then_inc(exped, 1)

            def pt_copy(s, b, u):
                pt_evacuate(act, copy, s, u)

            def r_copy(s, b, t):
                bank, use = t_use("r", t)
                act.wait_ge(t_full[bank], 4 * s + use + 1)
                wait(act, on_ready[t], s)
                copy(rb[:, t, :], TB[bank][:, :]).then_inc(t_free[bank], 1)

            def route_h(r):
                act.wait_ge(pe_h, r + 1)
                nc.scalar.activation(hfT[:], M0[:, T:2 * T], ACT.Identity, bias=lnb[:, 0:1], scale=lng[:, 0:1]).then_inc(act_h, 1)

            def route_base(r):
                act.wait_ge(hh_ready, r + 1)
                stand_alone(act, passed)
                for t in range(NT):
                    h = hall[:, bass.ds(r * NT + t, 1), :].rearrange("p a d -> p (a d)")
                    last = nc.scalar.activation(h, h, ACT.Identity, bias=rst[:, 7, t:t + 1], scale=rst[:, 8, t:t + 1])
                last.then_inc(base_ready, 1)

            def route_e(r):
                act.wait_ge(dlog_ready, r + 1)
                nc.scalar.activation(eg[:], dlog[:], ACT.Exp).then_inc(eg_ready, 1)

            def body(s, b):
                more = not isinstance(s, int) or s + 1 < B
                routed = not isinstance(s, int) or s > 0
                s1, b1_ = s + 1, 1 - b
                exps(s, b, 0)
                exps(s, b, 1)
                if more:
                    p_xT(s1, b1_)
                pt_copy(s, b, 1)
                exps(s, b, 2)
                r_copy(s, b, 0)
                if more:
                    p_sq(s1, b1_)
                exps(s, b, 3)
                if routed:
                    route_h(s - 1)
                pt_copy(s, b, 3)
                exps(s, b, 4)
                exps(s, b, 5)
                if more:
                    p_q(s1, b1_, 0)
                pt_copy(s, b, 5)
                if more:
                    p_ksq(s1)
                if more:
                    p_q(s1, b1_, 1)
                r_copy(s, b, 1)
                if more:
                    p_qT(s1, b1_, 0)
                if more:
                    p_qT(s1, b1_, 1)
                    p_kT(s1, b1_)
                if routed:
                    route_e(s - 1)
                    route_base(s - 1)

            p_xT(0, 0)
            p_sq(0, 0)
            p_q(0, 0, 0)
            p_ksq(0)
            p_q(0, 0, 1)
            p_qT(0, 0, 0)
            p_qT(0, 0, 1)
            p_kT(0, 0)
            for s in (0, 1, 2):
                body(s, s % 2)
            with act.Fori(1, 6) as i:
                body(i * 2 + 1, 1)
                body(i * 2 + 2, 0)
            for s in (13, 14, 15):
                body(s, s % 2)
            route_h(B - 1)
            route_e(B - 1)
            route_base(B - 1)
            pad_experts(act, range(E // 2, E))
            nc.scalar.activation(gelu_of_zero[:], zero8[:], ACT.Gelu)

            def gelu(j, b):
                act.wait_ge(biases_ready, j + 1)
                wait(act, y_done, j - 1)
                for half in range(2):
                    act.wait_ge(hidden_done, 2 * j + half + 1)
                    for c in range(2 * half, 2 * half + 2):
                        last = nc.scalar.activation(hid[:, b % 2, c, :], HID[b % 2][half][:, (c % 2) * GR:(c % 2 + 1) * GR],
                                                    ACT.Gelu, bias=b1c[:, b, c:c + 1])
                    last.then_inc(hid_ready, 1)

            for b in range(XR):
                gelu(b, b)
            with act.Fori(1, TURNS) as i:
                for b in range(XR):
                    gelu(i * XR + b, b)
            for b in range(LEFT):
                gelu(TURNS * XR + b, b)

        @block.vector
        def _(dve):
            dve.wait_ge(pool_init, 4)
            nc.vector.tensor_copy(identb[:], ident[:])
            nc.vector.tensor_copy(beforeb[:], before[:])
            nc.vector.tensor_scalar(region8[:], region8[:], float(P), None, ALU.mult)
            for j in range(4):
                nc.vector.tensor_copy(masks[:, j * P:(j + 1) * P], maskf[:])
            dve.wait_ge(consts_in, 16 * SMALL)
            nc.vector.tensor_scalar(wq[:], wq_raw[:].rearrange("p g k d -> p (g k d)"), qln[:, 0:1], None, ALU.mult)
            nc.vector.tensor_scalar(wkv[:], wkv_raw[:], kvln[:, 0:1], None, ALU.mult)
            nc.vector.tensor_tensor(khw[:], hw2[:, 0:1], hw2[:, 1:2], ALU.mult).then_inc(dve_init, 1)

            def table_chunk(n, u, i):
                dve.wait_ge(turned, 2 * n + 2)
                wait(dve, chunk_out[u], 16 * i)
                nc.vector.tensor_copy(w_out[:, u, 4:8, :].rearrange("p j d -> p (j d)"), banks[2 * (u % 4) + 1][:, :]).then_inc(odd_copied, 1)

            for u in range(RING):
                table_chunk(u, u, 0)
            with dve.Fori(1, ROUNDS) as i:
                for u in range(RING):
                    table_chunk(i * RING + u, u, i)
            table_chunk(CHUNKS - 1, 0, ROUNDS)

            def embed(s):
                dve.wait_ge(f_ready, s + 1)
                for t in range(NT):
                    last = nc.vector.bn_stats(bst[:, t, :], f[:, t, :])
                last.then_inc(e_dve, 1)
                dve.wait_ge(e_dve, s + 1)
                wait(dve, embedded, s)
                stand_alone(dve, passed)
                for t in range(NT):
                    last = nc.vector.bn_aggr(mv[:, t, :], bst[:, t, :])
                last.then_inc(mv_ready, 1)

            def embed_x(s, b):
                dve.wait_ge(embedded, s + 1)
                wait(dve, pe_xT, s - 1)
                for t in range(NT):
                    last = nc.vector.tensor_scalar(xn[:, b, t, :], f[:, t, :], est[:, 6, t:t + 1], est[:, 7, t:t + 1],
                                                   ALU.mult, ALU.subtract)
                last.then_inc(x_ready, 1)

            def copy(dst, src):
                return nc.vector.tensor_copy(dst, src)

            def p_stat(s, b):
                dve.wait_ge(pe_stat, s + 1)
                wait(dve, rq_ready, s)
                nc.vector.tensor_scalar(em[:].rearrange("p t c -> p (t c)"), M1[:, 0:2 * NT], 1e-6, None, ALU.add).then_inc(dve_stat, 1)

            def rotate(oa, ob, src, t_cos, t_sin):
                h = DR // 2
                nc.vector.tensor_tensor(oa, src, t_cos, ALU.mult)
                nc.vector.tensor_tensor(ob[..., 0:h], src[..., h:DR], t_sin[..., 0:h], ALU.mult)
                return nc.vector.tensor_tensor(ob[..., h:DR], src[..., 0:h], t_sin[..., h:DR], ALU.mult)

            def p_kv(s, b):
                dve.wait_ge(pe_kv, s + 1)
                wait(dve, k_ready, s)
                m = M0[:, :].rearrange("p (t c) -> p t c", t=NT)
                shape = [P, NT, KVH, DR]
                rotate(krope_a[:], krope_b[:], m[:, :, 192:256].rearrange("p t (k d) -> p t k d", k=KVH),
                       cossin[:, 0].unsqueeze(2).to_broadcast(shape), cossin[:, 1].unsqueeze(2).to_broadcast(shape))
                dve.wait_ge(skv_ready, s + 1)
                nc.vector.tensor_tensor(kt[:, :, :, 0:DN], m[:, :, 0:64].rearrange("p t (k d) -> p t k d", k=KVH),
                                        skv[:].unsqueeze(2).unsqueeze(3).to_broadcast(shape), ALU.mult)
                nc.vector.tensor_tensor(v[:, b], m[:, :, 64:192], skv[:].unsqueeze(2).to_broadcast([P, NT, KVH * HD]),
                                        ALU.mult).then_inc(dve_kv, 1)

            def p_rope(s, b, t):
                dve.wait_ge(act_q, NT * s + t + 1)
                wait(dve, q_ready[t], s)
                src = (M1, M0)[t][:, :].rearrange("p (h d) -> p h d", d=HD)[:, :, DN:HD]
                shape = [P, H, DR]
                rotate(rope_a[:, t], rope_b[:, t], src, cossin[:, 0, t].unsqueeze(1).to_broadcast(shape),
                       cossin[:, 1, t].unsqueeze(1).to_broadcast(shape)).then_inc(dve_rope, 1)
                if t == 1:
                    dve.wait_ge(dve_rope, NT * s + NT)
                    nc.vector.tensor_tensor(qt[:, 1].rearrange("p g k d -> p (g k) d")[:, :, DN:HD], rope_a[:, 1], rope_b[:, 1],
                                            ALU.add).then_inc(q_ready[1], 1)

            def p_kss(s):
                dve.wait_ge(ksq_ready, s + 1)
                nc.vector.reduce_sum(kss[:], ksq[:].rearrange("p t k d -> p (t k) d"), AX.X).then_inc(kss_ready, 1)

            def p_qss(s):
                dve.wait_ge(act_q, NT * s + NT)
                nc.vector.reduce_sum(qss[:].rearrange("p t h -> p (t h)"), qsq[:].rearrange("p t h d -> p (t h) d"), AX.X).then_inc(qss_ready, 1)

            def bias(s, b, u):
                t, kv, j0, n = UNITS[u]
                dve.wait_ge(scored, NU * s + u + 1)
                nc.vector.tensor_reduce(negmax[:, u, 0:n], S[u % 3][:, :].rearrange("p (c k) -> p c k", c=n), AX.X, ALU.max,
                                        negate=True).then_inc(max_done, 1)
                dve.wait_ge(max_done, NU * s + u + 1)
                if u == 0:
                    dve.wait_ge(rq_ready, s + 1)
                nc.vector.tensor_tensor(nbias[:, u, 0:n], negmax[:, u, 0:n], rq[:, b, t, j0:j0 + n, kv], ALU.mult).then_inc(bias_ready, 1)

            def recip(s, t):
                dve.wait_ge(exped, NU * s + (2, NU)[t])
                nc.vector.reciprocal(rinv[:, t].rearrange("p g k -> p (g k)"), rsum[:, t].rearrange("p g k -> p (g k)")).then_inc(rinv_done, 1)
                dve.wait_ge(rinv_done, NT * s + t + 1)
                nc.vector.tensor_copy(rwide[:, t].rearrange("p g (k d) -> p (g k) d", k=KVH),
                                      rinv[:, t].rearrange("p g k -> p (g k)").unsqueeze(2).to_broadcast([P, H, HD])).then_inc(rinv_ready, 1)

            def normalise(s, t):
                bank, use = t_use("r", t)
                dve.wait_ge(pv_done[t], s + 1)
                dve.wait_ge(t_free[bank], 4 * s + use + 1)
                wait(dve, pe_wo, NT * s)
                nc.vector.tensor_tensor(on[:, t].rearrange("p j q -> p (j q)"), O[:, :], rb[:, t, :], ALU.mult).then_inc(on_ready[t], 1)

            def residual(s):
                dve.wait_ge(pe_wo, NT * (s + 1))
                h = hall[:, bass.ds(s * NT, NT), :]
                nc.vector.tensor_tensor(h, O[:, 0:NT * D].rearrange("p (t d) -> p t d", t=NT), h, ALU.add).then_inc(h_added, 1)

            STATS_STEPS = 5

            def route_stats(r):
                dve.wait_ge(h_added, r + 1)
                stand_alone(dve, passed)
                for t in range(NT):
                    last = nc.vector.bn_stats(bst2[:, t, :], hall[:, bass.ds(r * NT + t, 1), :].rearrange("p a d -> p (a d)"))
                k = [0]

                def link(ins):
                    k[0] += 1
                    ins.then_inc(r_stats, 1)
                    dve.wait_ge(r_stats, STATS_STEPS * r + k[0])

                link(last)
                stand_alone(dve, passed)
                for t in range(NT):
                    last = nc.vector.bn_aggr(mv2[:, t, :], bst2[:, t, :])
                last.then_inc(r_stats, 1)
                assert k[0] == 1

            def route_variances(r):
                k = [2]

                def link(ins):
                    k[0] += 1
                    ins.then_inc(r_stats, 1)
                    dve.wait_ge(r_stats, STATS_STEPS * r + k[0])

                dve.wait_ge(r_stats, STATS_STEPS * r + 2)
                link(nc.vector.tensor_scalar(rst[:, 0, :], mv2[:, :, 1], 1e-5, None, ALU.add))
                link(nc.vector.reciprocal(rst[:, 4, :], rst[:, 0, :]))
                link(nc.vector.tensor_tensor(rst[:, 4, :], rst[:, 4, :], mv2[:, :, 1], ALU.mult))
                nc.vector.tensor_scalar(rst[:, 1, :], rst[:, 4, :], 1e-5, None, ALU.add).then_inc(mv2_ready, 1)
                assert k[0] == STATS_STEPS

            def route_hh(r, b, half):
                dve.wait_ge(coef_ready, r + 1)
                wait(dve, scattered[b], 16 * NT * K * half)
                h = [hall[:, bass.ds(r * NT + t, 1), :].rearrange("p a d -> p (a d)") for t in range(NT)]
                for t in range(NT):
                    last = nc.vector.tensor_scalar(row[:, b, t, :, 0:D], h[t].unsqueeze(1).to_broadcast([P, K, D]),
                                                   rst[:, 5, t:t + 1], rst[:, 6, t:t + 1], ALU.mult, ALU.subtract)
                last.then_inc(hh_ready, 1)

            TOP_STEPS = 4

            def route_logits(r):
                dve.wait_ge(pe_logits, r + 1)
                nc.vector.tensor_tensor(lg[:], M1[:, 4:4 + NT * E].rearrange("p (t e) -> p t e", t=NT),
                                        br[:].unsqueeze(1).to_broadcast([P, NT, E]), ALU.add).then_inc(logits_copied, 1)

            def route_top(r):
                k = [0]

                def link(ins):
                    k[0] += 1
                    ins.then_inc(r_dve, 1)
                    dve.wait_ge(r_dve, TOP_STEPS * r + k[0])

                dve.wait_ge(logits_copied, r + 1)
                stand_alone(dve, passed)
                nc.vector.max(mx8[:, 0], lg[:, 0])
                link(nc.vector.max(mx8[:, 1], lg[:, 1]))
                stand_alone(dve, passed)
                nc.vector.max_index(ix8[:, 0], mx8[:, 0], lg[:, 0])
                link(nc.vector.max_index(ix8[:, 1], mx8[:, 1], lg[:, 1]))
                nc.vector.tensor_tensor(dlog[:], mx8[:, :, 1], mx8[:, :, 0], ALU.subtract).then_inc(dlog_ready, 1)
                link(nc.vector.tensor_copy(ixf[:], ix8[:, :, 0:K]))
                shape = [P, NT * K, E]
                link(nc.vector.tensor_tensor(chosen[:].rearrange("p t k e -> p (t k) e"),
                                             ixf[:].rearrange("p t k -> p (t k)").unsqueeze(2).to_broadcast(shape),
                                             iota8[:].unsqueeze(1).to_broadcast(shape), ALU.is_equal))
                nc.vector.tensor_tensor(both[:], chosen[:, :, 0], chosen[:, :, 1], ALU.add).then_inc(both_ready, 1)
                assert k[0] == TOP_STEPS

            GATE_STEPS = 2

            def route_gates(r, b):
                dve.wait_ge(eg_ready, r + 1)
                nc.vector.tensor_scalar(eg1[:], eg[:], 1.0, None, ALU.add).then_inc(g_dve, 1)
                dve.wait_ge(g_dve, GATE_STEPS * r + 1)
                nc.vector.reciprocal(row[:, b, :, 0, GATE], eg1[:]).then_inc(g_dve, 1)
                dve.wait_ge(g_dve, GATE_STEPS * r + 2)
                nc.vector.tensor_tensor(row[:, b, :, 1, GATE], eg[:], row[:, b, :, 0, GATE], ALU.mult)

            SLOT_STEPS = 4

            def route_slots(r, b):
                k = [0]

                def link(ins):
                    k[0] += 1
                    ins.then_inc(c_dve, 1)
                    dve.wait_ge(c_dve, SLOT_STEPS * r + k[0])

                dve.wait_ge(pe_rank, r + 1)
                nc.vector.tensor_tensor(pos[:], M1[:, T:T + NT * E].rearrange("p (t e) -> p t e", t=NT),
                                        region8[:].unsqueeze(1).to_broadcast([P, NT, E]), ALU.add).then_inc(rank_copied, 1)
                dve.wait_ge(rank_copied, r + 1)
                link(nc.vector.tensor_tensor(posk[:], chosen[:], pos[:].unsqueeze(2).to_broadcast([P, NT, K, E]), ALU.mult))
                link(nc.vector.reduce_sum(slotf[:], posk[:].rearrange("p t k e -> p (t k) e"), AX.X))
                nc.vector.tensor_copy(slot[:, b], slotf[:]).then_inc(slot_ready, 1)
                for t in range(NT):
                    link(nc.vector.tensor_tensor(seen[:], seen[:], both[:, t], ALU.add))
                assert k[0] == SLOT_STEPS

            def body(s, b, half):
                more = not isinstance(s, int) or s + 1 < B
                routed = not isinstance(s, int) or s > 0
                more2 = not isinstance(s, int) or s + 2 < B
                s1, b1_ = s + 1, 1 - b
                bias(s, b, 0)
                bias(s, b, 1)
                if routed:
                    residual(s - 1)
                    route_stats(s - 1)
                if more:
                    embed_x(s1, b1_)
                pt_evacuate(dve, copy, s, 0)
                bias(s, b, 2)
                recip(s, 0)
                if routed:
                    route_variances(s - 1)
                bias(s, b, 3)
                if more2:
                    embed(s + 2)
                if routed:
                    route_hh(s - 1, 1 - b, half)
                if more:
                    p_stat(s1, b1_)
                pt_evacuate(dve, copy, s, 2)
                normalise(s, 0)
                bias(s, b, 4)
                if routed:
                    route_logits(s - 1)
                bias(s, b, 5)
                if more:
                    p_kv(s1, b1_)
                pt_evacuate(dve, copy, s, 4)
                recip(s, 1)
                if more:
                    p_rope(s1, b1_, 0)
                if more:
                    p_kss(s1)
                if more:
                    p_rope(s1, b1_, 1)
                if more:
                    p_qss(s1)
                normalise(s, 1)
                if routed:
                    route_top(s - 1)
                    route_gates(s - 1, 1 - b)
                    route_slots(s - 1, 1 - b)

            embed(0)
            embed_x(0, 0)
            p_stat(0, 0)
            p_kv(0, 0)
            p_rope(0, 0, 0)
            p_kss(0)
            p_rope(0, 0, 1)
            p_qss(0)
            embed(1)
            for s in (0, 1, 2):
                body(s, s % 2, (s - 1) // 2)
            with dve.Fori(1, 6) as i:
                body(i * 2 + 1, 1, i)
                body(i * 2 + 2, 0, i)
            for s in (13, 14, 15):
                body(s, s % 2, (s - 1) // 2)
            residual(B - 1)
            route_stats(B - 1)
            route_variances(B - 1)
            r = B - 1
            route_hh(r, 1, r // 2)
            route_logits(r)
            route_top(r)
            route_gates(r, 1)
            route_slots(r, 1)

            k = [0]

            def then(ins):
                k[0] += 1
                ins.then_inc(t_dve, 1)
                dve.wait_ge(t_dve, k[0])

            dve.wait_ge(pe_count, 1)
            je_shape = [1, NJ, E]
            region, experts = region8[0:1, :], iota8[0:1, :]
            then(nc.vector.tensor_copy(cnt[:], M1[0:1, 2 * T - E:2 * T]))
            then(nc.vector.tensor_tensor(padrow[:], region, cnt[:], ALU.add))
            nc.vector.tensor_copy(pad_i[:], padrow[:]).then_inc(pads_known, 1)
            then(nc.vector.tensor_scalar(cnti[:], cnt[:], float(GR - 1), None, ALU.add))
            then(nc.vector.tensor_scalar(cntt[:], cnti[:], GR.bit_length() - 1, None, ALU.logical_shift_right))
            then(nc.vector.tensor_copy(ntile[:], cntt[:]))
            then(nc.vector.tensor_tensor_scan(tend[:], ntile[:], zero8[:], 0.0, ALU.add, ALU.add))
            then(nc.vector.tensor_tensor(tbase[:], tend[:], ntile[:], ALU.subtract))
            then(nc.vector.scalar_tensor_tensor(tbase[:], tbase[:], -float(GR), region, ALU.mult, ALU.add))
            then(nc.vector.tensor_tensor(je[:], iotaj[:].unsqueeze(2).to_broadcast(je_shape),
                                         tend[:].unsqueeze(1).to_broadcast(je_shape), ALU.is_ge))
            then(nc.vector.reduce_sum(jexp[:], je[:], AX.X))
            then(nc.vector.tensor_tensor(je[:], jexp[:].unsqueeze(2).to_broadcast(je_shape),
                                         experts.unsqueeze(1).to_broadcast(je_shape), ALU.is_equal))
            then(nc.vector.tensor_tensor(je[:], je[:], tbase[:].unsqueeze(1).to_broadcast(je_shape), ALU.mult))
            then(nc.vector.reduce_sum(jstart[:], je[:], AX.X))
            then(nc.vector.scalar_tensor_tensor(jstart[:], iotaj[:], float(GR), jstart[:], ALU.mult, ALU.add))
            then(nc.vector.tensor_scalar(jvalid[:], jexp[:], float(E), None, ALU.is_lt))
            then(nc.vector.tensor_scalar(jstart[:], jstart[:], cnt[:, 0:1], None, ALU.subtract))
            then(nc.vector.tensor_tensor(jstart[:], jstart[:], jvalid[:], ALU.mult))
            then(nc.vector.tensor_scalar(start_i[:], jstart[:], cnt[:, 0:1], None, ALU.add))
            nc.vector.tensor_tensor(expert_i[:], jexp[:], jvalid[:], ALU.mult).then_inc(tables_ready, 1)

            def take_biases(j, b):
                e = dve.value_load(expert_i[0:1, bass.ds(j, 1)], min_val=0, max_val=E - 1)
                wait(dve, hid_ready, 2 * (j - XR + 1))
                nc.vector.tensor_copy(b2c[:, b, :], b2s[:, bass.ds(e, 1), :].rearrange("p a f -> p (a f)"))
                nc.vector.tensor_copy(b1c[:, b, :], b1s[:, bass.ds(e, 1), :].rearrange("p a f -> p (a f)")).then_inc(biases_ready, 1)

            def take_rows(j, b, turn):
                dve.wait_ge(x_turned, j + 1)
                wait(dve, hidden_done, 2 * (j - 1))
                nc.vector.tensor_scalar(hT[:, b % 2, :], XT[b % 2][:, 0:GR], lng[:, 0:1], lnb[:, 0:1], ALU.mult, ALU.add).then_inc(hT_ready, 1)
                wait(dve, y_out[b], 16 * GT * turn)
                nc.vector.tensor_copy(where[:, b, :], rows[:, b, :, DEST])

            def give_y(j, b):
                dve.wait_ge(y_done, j + 1)
                nc.vector.tensor_tensor(yt[:, b % 2], Y[b % 2][:, 0:GT * D].rearrange("p (t d) -> p t d", t=GT),
                                        b2c[:, b].unsqueeze(1).to_broadcast([P, GT, D]), ALU.add).then_inc(y_biased, 1)
                dve.wait_ge(y_biased, j + 1)
                for t in range(GT):
                    last = nc.vector.tensor_scalar(yb[:, b, t, :], yt[:, b % 2, t, :], rows[:, b, t, GATE:GATE + 1], None, ALU.mult)
                last.then_inc(y_ready, 1)

            def expert_steps(i):
                for b in range(LEFT if isinstance(i, int) and i == TURNS else XR):
                    ahead, b2_ = i * XR + b + 2, (b + 2) % XR
                    if not isinstance(i, int) or ahead < NJ:
                        take_rows(ahead, b2_, i + (b + 2) // XR)
                        take_biases(ahead, b2_)
                    give_y(i * XR + b, b)

            dve.wait_ge(weights_in, 32)
            for b in range(2):
                take_rows(b, b, 0)
                take_biases(b, b)
            expert_steps(0)
            with dve.Fori(1, TURNS) as i:
                expert_steps(i)
            expert_steps(TURNS)

            dve.wait_ge(base_ready, B)
            for c in range(OC):
                h = hall[:, c * QT:(c + 1) * QT, :]
                dve.wait_ge(y_in[c], 32)
                nc.vector.tensor_tensor(h, h, y_parts[:, 0, c], ALU.add).then_inc(y_add, 1)
                dve.wait_ge(y_add, c + 1)
                nc.vector.tensor_tensor(h, h, y_parts[:, 1, c], ALU.add).then_inc(y_sum, 1)

        @block.tensor
        def _(pe):
            mm = nc.tensor.matmul
            pe.wait_ge(pool_init, 4)

            def table_chunk(n, u, i):
                pe.wait_ge(chunk_in[u], 16 * (i + 1))
                wait(pe, even_copied, n - 3)
                wait(pe, odd_copied, n - 3)
                w = w_in[:, u, :].rearrange("p (c j) -> p j c", j=CJ)
                for j in range(CJ):
                    last = nc.tensor.transpose(banks[2 * (u % 4) + j // 4][:, (j % 4) * P:(j % 4 + 1) * P], w[:, j], ident[:])
                    if j % 4 == 3:
                        last.then_inc(turned, 1)

            for u in range(RING):
                table_chunk(u, u, 0)
            with pe.Fori(1, ROUNDS) as i:
                for u in range(RING):
                    table_chunk(i * RING + u, u, i)
            table_chunk(CHUNKS - 1, 0, ROUNDS)
            pe.wait_ge(chunk_in[1], 16 * (ROUNDS + 1))
            pe.wait_ge(even_copied, CHUNKS - 3)
            pe.wait_ge(odd_copied, CHUNKS - 3)
            nc.tensor.transpose(banks[2][0:TAIL, 0:D], w_in[:, 1, 0:TAIL], ident[:]).then_inc(turned, 1)

            pe.wait_ge(even_copied, CHUNKS + 1)
            pe.wait_ge(odd_copied, CHUNKS)
            pe.wait_ge(consts_in, 16 * SMALL)
            pe.wait_ge(dve_init, 1)
            for j in range(G):
                w = wvr[:, j].rearrange("p a d -> p (a d)")
                last = nc.tensor.transpose(banks[0][:, j * P:(j + 1) * P], w, ident[:])
            last.then_inc(setup_pe, 1)
            pe.wait_ge(setup_act, 1)
            for j in range(G):
                last = mm(banks[1][:, 0:D], wvrT[:, j, :], wo[:, j, :], start=(j == 0), stop=(j == G - 1))
            last.then_inc(setup_pe, 1)
            pe.wait_ge(setup_act, 2)

            def p_a(s, b):
                pe.wait_ge(x_ready, s + 1)
                wait(pe, act_qT, NT * s)
                for t in range(NT):
                    last = nc.tensor.transpose(M0[:, t * P:(t + 1) * P], xn[:, b, t, :], ident[:])
                last.then_inc(pe_xT, 1)

            def p_b(s, b):
                pe.wait_ge(act_xT, s + 1)
                wait(pe, act_kT, s)
                wait(pe, rank_copied, s - 2)
                mm(M1[0:RQ, 0:T], wdq[:], xT[:, b, :], start=True, stop=True)
                mm(M1[:, T:2 * T], wdkv[:], xT[:, b, :], start=True, stop=True).then_inc(pe_c, 1)

            def p_stats(s, b):
                pe.wait_ge(act_sq, s + 1)
                for t in range(NT):
                    tok = slice(t * P, (t + 1) * P)
                    mm(M1[:, 2 * t:2 * t + 1], sqc[0:RQ, 0, tok], mean_w[0:RQ, 0:1], start=True, stop=True)
                    last = mm(M1[:, 2 * t + 1:2 * t + 2], sqc[:, 1, tok], mean_w[:, 1:2], start=True, stop=True)
                last.then_inc(pe_stat, 1)

            def route_turn(r, b):
                pe.wait_ge(hh_ready, r + 1)
                wait(pe, act_h, r)
                wait(pe, act_qT, min(NT * (r + 2), NT * B) if isinstance(r, int) else NT * (r + 2))
                for t in range(NT):
                    last = nc.tensor.transpose(M0[:, T + t * P:T + (t + 1) * P], row[:, b, t, 0, 0:D], ident[:])
                last.then_inc(pe_h, 1)

            def route_logits(r):
                pe.wait_ge(act_h, r + 1)
                wait(pe, rank_copied, r)
                pe.wait_ge(dve_stat, min(r + 3, B) if isinstance(r, int) else r + 3)
                for t in range(NT):
                    last = mm(M1[:, 4 + E * t:4 + E * (t + 1)], hfT[:, t * P:(t + 1) * P], wrT[:], start=True, stop=True)
                last.then_inc(pe_logits, 1)

            def route_rank(r):
                pe.wait_ge(both_ready, r + 1)
                pe.wait_ge(act_kT, min(r + 3, B) if isinstance(r, int) else r + 3)
                for t in range(NT):
                    dst = M1[:, T + E * t:T + E * (t + 1)]
                    mm(dst, beforeb[:], both[:, t, :], start=True, stop=False)
                    if t > 0:
                        mm(dst, onesb[:], both[:, 0, :], start=False, stop=False)
                    last = mm(dst, onesb[:], seen[:], start=False, stop=True)
                last.then_inc(pe_rank, 1)

            def p_kvm(s, b):
                for t in range(NT):
                    tok = slice(t * P, (t + 1) * P)
                    mm(M0[:, t * T:t * T + 192], ckvT[:, tok], wkv[:], start=True, stop=True)
                    last = mm(M0[:, t * T + 192:(t + 1) * T], xT[:, b, tok], wkr[:], start=True, stop=True)
                last.then_inc(pe_kv, 1)

            def p_q(s, b, t):
                if t == 0:
                    pe.wait_ge(dve_stat, s + 1)
                    wait(pe, logits_copied, s - 1)
                else:
                    pe.wait_ge(dve_kv, s + 1)
                mm((M1, M0)[t][:, :], cqT[:, t * P:(t + 1) * P], wq[:], start=True, stop=True).then_inc(pe_q, 1)

            def p_qT(s, b, t):
                pe.wait_ge(act_q, NT * s + t + 1)
                pe.wait_ge(q_ready[t], s + 1)
                for j in range(G):
                    last = nc.tensor.transpose((M1, M0)[t][:, j * P:(j + 1) * P], qt[:, t, j].rearrange("p k d -> p (k d)"), ident[:])
                last.then_inc(pe_qT, 1)

            def p_kT(s, b):
                pe.wait_ge(k_ready, s + 1)
                pe.wait_ge(act_qT, NT * s + 1)
                for t in range(NT):
                    last = nc.tensor.transpose(M1[:, t * P:(t + 1) * P], kt[:, t].rearrange("p k d -> p (k d)"), ident[:])
                last.then_inc(pe_kT, 1)

            def scores(s, b, u):
                t, kv, j0, n = UNITS[u]
                if u == 0:
                    pe.wait_ge(act_kT, s + 1)
                    pe.wait_ge(act_qT, NT * s + NT)
                wait(pe, exped, NU * s + u - 2)
                bank = S[u % 3]
                w = P * (t + 1)
                rows = slice(kv * HD, kv * HD + HD)
                for c in range(n):
                    mm(bank[:, c * w:(c + 1) * w], qT[rows, b, t, j0 + c, :], kT[rows, b, 0:w],
                       start=(c == 0), stop=True, skip_group_check=True)
                last = mm(bank[:, :].rearrange("p (c k) -> p c k", c=n)[:, :, w - P:w], identb[:],
                          masks[:, 0:n * P].rearrange("p (c k) -> p c k", c=n), start=False, stop=True, skip_group_check=True)
                last.then_inc(scored, 1)

            def turn(s, b, u):
                bank, use = t_use("p", u)
                pe.wait_ge(exped, NU * s + u + 1)
                wait(pe, t_free[bank], 4 * s + use)
                for c in range(4):
                    last = nc.tensor.transpose(TB[bank][:, c * P:(c + 1) * P], pm[:, u % 2, c * P:(c + 1) * P], ident[:])
                last.then_inc(t_full[bank], 1)

            def spread(s, b, t):
                bank, use = t_use("r", t)
                pe.wait_ge(rinv_ready, NT * s + t + 1)
                wait(pe, t_free[bank], 4 * s + use)
                for j in range(G):
                    last = nc.tensor.transpose(TB[bank][:, j * P:(j + 1) * P],
                                               rwide[:, t, j], ident[:])
                last.then_inc(t_full[bank], 1)

            def pv(s, b, t):
                for bank in range(2):
                    pe.wait_ge(t_free[bank], 4 * s + (1, 4 - bank)[t])
                if t == 0:
                    wait(pe, h_added, s)
                else:
                    pe.wait_ge(on_ready[0], s + 1)
                for kb in range(t + 1):
                    for kv in range(KVH):
                        rows = slice(kv * HD, kv * HD + HD)
                        rhs = pt0[:, kv] if t == 0 else pt1[:, kv, :, kb, :]
                        last = mm(O[rows, :], v[:, b, kb, rows], rhs, start=(kb == 0), stop=(kb == t))
                last.then_inc(pv_done[t], 1)

            def w_out_mm(s, b, t):
                pe.wait_ge(on_ready[1], s + 1)
                dst = O[:, t * D:(t + 1) * D]
                for j in range(G):
                    mm(dst, on[:, t, j, :], wo[:, j, :], start=(j == 0), stop=False)
                mm(dst, xT[:, b, t * P:(t + 1) * P], wvo[:], start=False, stop=True).then_inc(pe_wo, 1)

            def body(s, b):
                more = not isinstance(s, int) or s + 1 < B
                s1, b1_ = s + 1, 1 - b
                routed = not isinstance(s, int) or s > 0
                if routed:
                    w_out_mm(s - 1, 1 - b, 0)
                if not isinstance(s, int) or s > 1:
                    route_rank(s - 2)
                scores(s, b, 0)
                scores(s, b, 1)
                if routed:
                    w_out_mm(s - 1, 1 - b, 1)
                scores(s, b, 2)
                turn(s, b, 0)
                scores(s, b, 3)
                if more:
                    p_a(s1, b1_)
                turn(s, b, 1)
                if more:
                    p_b(s1, b1_)
                spread(s, b, 0)
                pv(s, b, 0)
                turn(s, b, 2)
                scores(s, b, 4)
                if more:
                    p_stats(s1, b1_)
                if routed:
                    route_turn(s - 1, 1 - b)
                turn(s, b, 3)
                scores(s, b, 5)
                if routed:
                    route_logits(s - 1)
                if more:
                    p_kvm(s1, b1_)
                if more:
                    p_q(s1, b1_, 0)
                turn(s, b, 4)
                turn(s, b, 5)
                if more:
                    p_q(s1, b1_, 1)
                spread(s, b, 1)
                pv(s, b, 1)
                if more:
                    p_qT(s1, b1_, 0)
                if more:
                    p_qT(s1, b1_, 1)
                if more:
                    p_kT(s1, b1_)

            p_a(0, 0)
            p_b(0, 0)
            p_stats(0, 0)
            p_kvm(0, 0)
            p_q(0, 0, 0)
            p_q(0, 0, 1)
            p_qT(0, 0, 0)
            p_qT(0, 0, 1)
            p_kT(0, 0)
            for s in (0, 1, 2):
                body(s, s % 2)
            with pe.Fori(1, 6) as i:
                body(i * 2 + 1, 1)
                body(i * 2 + 2, 0)
            for s in (13, 14, 15):
                body(s, s % 2)
            r = B - 1
            w_out_mm(r, 1, 0)
            route_rank(r - 1)
            w_out_mm(r, 1, 1)
            route_turn(r, 1)
            route_logits(r)
            route_rank(r)
            pe.wait_ge(c_dve, 4 * B)
            mm(M1[:, 2 * T - E:2 * T], onesb[:], seen[:], start=True, stop=True).then_inc(pe_count, 1)

            pe.wait_ge(tables_ready, 1)

            def turn_rows(j, b, turn):
                pe.wait_ge(group_in[b], 16 * (turn + 1))
                wait(pe, hT_ready, j - 1)
                for t in range(GT):
                    last = nc.tensor.transpose(XT[b % 2][:, t * P:(t + 1) * P], rows[:, b, t, 0:D], ident[:])
                last.then_inc(x_turned, 1)

            def up(j, b, turn):
                pe.wait_ge(w1_in[b], 16 * (turn + 1))
                pe.wait_ge(hT_ready, j + 1)
                for half in range(2):
                    wait(pe, hid_ready, 2 * (j - 2) + half + 1)
                    for c in range(2 * half, 2 * half + 2):
                        last = mm(HID[b % 2][half][:, (c % 2) * GR:(c % 2 + 1) * GR], w1c[:, b, c * P:(c + 1) * P],
                                  hT[:, b % 2, :], start=True, stop=True)
                    last.then_inc(hidden_done, 1)

            def down(j, b):
                e = pe.value_load(expert_i[0:1, bass.ds(j, 1)], min_val=0, max_val=E - 1)
                pe.wait_ge(hid_ready, 2 * j + 2)
                wait(pe, y_biased, j - 1)
                for t in range(GT):
                    for c in range(FC):
                        last = mm(Y[b % 2][:, t * D:(t + 1) * D], hid[:, b % 2, c, t * P:(t + 1) * P],
                                  w2s[:, bass.ds(e, 1), c, :].rearrange("p a d -> p (a d)"), start=(c == 0), stop=(c == FC - 1))
                last.then_inc(y_done, 1)

            def expert_steps(i):
                for b in range(LEFT if isinstance(i, int) and i == TURNS else XR):
                    j = i * XR + b
                    if not isinstance(i, int) or j + 2 < NJ:
                        turn_rows(j + 2, (b + 2) % XR, i + (b + 2) // XR)
                    if not isinstance(i, int) or j + 1 < NJ:
                        up(j + 1, (b + 1) % XR, i + (b + 1) // XR)
                    down(j, b)

            pe.wait_ge(weights_in, 32)
            turn_rows(0, 0, 0)
            turn_rows(1, 1, 0)
            up(0, 0, 0)
            expert_steps(0)
            with pe.Fori(1, TURNS) as i:
                expert_steps(i)
            expert_steps(TURNS)


_INS = ['x', 'L0_tok_W', 'L0_tok_b', 'L0_attn_W_DQ', 'L0_attn_W_UQ', 'L0_attn_W_QR', 'L0_attn_W_DKV', 'L0_attn_W_UK',
        'L0_attn_W_UV', 'L0_attn_W_KR', 'L0_attn_W_VR', 'L0_attn_W_O', 'L0_attn_q_ln_w', 'L0_attn_kv_ln_w',
        'L0_attn_q_head_norm_w', 'L0_attn_k_head_norm_w', 'L0_ffn_ln_g', 'L0_ffn_ln_b', 'L0_ffn_w_r', 'L0_ffn_b_r',
        'L0_ffn_W1', 'L0_ffn_b1', 'L0_ffn_W2', 'L0_ffn_b2']


def _rope_table(np):
    inv_freq = 1.0 / 500000.0 ** (np.arange(0, DR, 2, dtype=np.float32) / DR)
    freqs = np.outer(np.arange(T, dtype=np.float32), inv_freq)
    emb = np.concatenate([freqs, freqs], axis=-1)
    sign = np.concatenate([-np.ones(DR // 2, np.float32), np.ones(DR // 2, np.float32)])
    both = np.stack([np.cos(emb), np.sin(emb) * sign]).astype(np.float32)
    return np.ascontiguousarray(both.reshape(2, NT, P, DR).transpose(2, 0, 1, 3))


def kernel(**inputs):
    import numpy as _np
    import concourse.bacc as _bacc
    from concourse import mybir as _mybir
    from concourse.bass_utils import run_bass_kernel_spmd as _run

    nc = _bacc.Bacc("TRN2", target_bir_lowering=False, num_devices=1)
    arrays, args = {}, []
    host = {name: _np.ascontiguousarray(inputs[name]) for name in _INS}
    host["rope"] = _rope_table(_np)
    for name, a in host.items():
        arrays[f"in_{name}_dram"] = a
        args.append(nc.dram_tensor(f"in_{name}_dram", a.shape, _mybir.dt.from_np(a.dtype), kind="ExternalInput").ap())
    table = nc.dram_tensor("row_table", (VOCAB, D), _mybir.dt.float32, kind="Internal").ap()
    xs = nc.dram_tensor("expert_rows", (E * REGION, ROW), _mybir.dt.float32, kind="Internal").ap()
    ys = nc.dram_tensor("expert_outputs", (K * N, D), _mybir.dt.float32, kind="Internal").ap()
    out = nc.dram_tensor("out_0_dram", (B, T, D), _mybir.dt.float32, kind="ExternalOutput").ap()
    tower_kernel(nc, *args, table, xs, ys, out)
    r = _run(nc, [arrays], core_ids=[0])
    return r.results[0]["out_0_dram"]
```
